# Optimizing a Trainium2 kernel written in Bass

```python
import numpy as np
import jax
import jax.numpy as jnp

def _softmax(x, axis=-1):
    return jax.nn.softmax(x, axis=axis)

def _gelu(x):
    return jax.nn.gelu(x, approximate=True)

def _silu(x):
    return jax.nn.silu(x)

def _sigmoid(x):
    return jax.nn.sigmoid(x)

def _layernorm(x, axis=-1, eps=1e-05):
    m = jnp.mean(x, axis=axis, keepdims=True)
    v = jnp.var(x, axis=axis, keepdims=True)
    return (x - m) / jnp.sqrt(v + eps)

def _scatter_add(tgt, idx, src, axis=0):
    return tgt.at[idx].add(src)

def _segment_sum(src, seg, n):
    return jax.ops.segment_sum(src, seg, n)
kernel_name = 'mk_prb_d2_jaxref_r8_40df3d'

def setup_inputs(seed: int=0):
    np.random.seed(seed)
    _w = jnp.asarray

    def _L0_attn_setup():
        import jax, jax.numpy as jnp
        import numpy as np
        STATE_SIZE = 16
        HIDDEN = 256
        DT_RANK = 64
        BATCH = 2
        SEQ = 256
        key = jax.random.key(seed)
        ks = jax.random.split(key, 8)
        scale = lambda fan_in: 1.0 / np.sqrt(fan_in)
        inp = {'input': jax.random.normal(ks[0], (BATCH, SEQ, HIDDEN), dtype=jnp.float32), 'W_dt_in': jax.random.uniform(ks[1], (DT_RANK, HIDDEN), jnp.float32, -scale(HIDDEN), scale(HIDDEN)), 'W_dt_out': jax.random.uniform(ks[2], (HIDDEN, DT_RANK), jnp.float32, -scale(DT_RANK), scale(DT_RANK)), 'b_dt_out': jax.random.uniform(ks[3], (HIDDEN,), jnp.float32, -scale(DT_RANK), scale(DT_RANK)), 'W_B': jax.random.uniform(ks[4], (STATE_SIZE, HIDDEN), jnp.float32, -scale(HIDDEN), scale(HIDDEN)), 'W_C': jax.random.uniform(ks[5], (STATE_SIZE, HIDDEN), jnp.float32, -scale(HIDDEN), scale(HIDDEN)), 'D': jax.random.normal(ks[6], (HIDDEN,), dtype=jnp.float32), 'A_log': jnp.log(jnp.tile(jnp.arange(1, STATE_SIZE + 1, dtype=jnp.float32), (HIDDEN, 1)))}
        return inp
    _L0_attn_in = _L0_attn_setup()

    def _L0_ffn_setup():
        import jax, jax.numpy as jnp
        import numpy as np
        D_MODEL = 256
        D_EXPERT = 1024
        EPS = 1e-08

        def ternary_quant(w):
            scale = jnp.mean(jnp.abs(w)) + EPS
            q = jnp.clip(jnp.round(w / scale), -1.0, 1.0) * scale
            return w + jax.lax.stop_gradient(q - w)
        key = jax.random.key(seed)
        k_x, k_up, k_gate, k_down = jax.random.split(key, 4)
        std_in = 1.0 / np.sqrt(D_MODEL)
        std_exp = 1.0 / np.sqrt(D_EXPERT)
        return {'x': jax.random.normal(k_x, (4, 256, D_MODEL), dtype=jnp.float32), 'W_up': jax.random.normal(k_up, (D_EXPERT, D_MODEL), dtype=jnp.float32) * std_in, 'W_gate': jax.random.normal(k_gate, (D_EXPERT, D_MODEL), dtype=jnp.float32) * std_in, 'W_down': jax.random.normal(k_down, (D_MODEL, D_EXPERT), dtype=jnp.float32) * std_exp}
    _L0_ffn_in = _L0_ffn_setup()

    def _L1_attn_setup():
        import jax, jax.numpy as jnp
        import numpy as np
        D_MODEL = 256
        NUM_HEADS = 16
        D_K = D_MODEL // NUM_HEADS

        def _heads(t, B, S):
            return t.reshape(B, S, NUM_HEADS, D_K).transpose(0, 2, 1, 3)
        key = jax.random.key(seed)
        ks = jax.random.split(key, 9)
        s = 1.0 / np.sqrt(D_MODEL)
        x = jax.random.normal(ks[0], (4, 512, D_MODEL), dtype=jnp.float32)
        wq = jax.random.uniform(ks[1], (D_MODEL, D_MODEL), jnp.float32, -s, s)
        bq = jax.random.uniform(ks[2], (D_MODEL,), jnp.float32, -s, s)
        wk = jax.random.uniform(ks[3], (D_MODEL, D_MODEL), jnp.float32, -s, s)
        bk = jax.random.uniform(ks[4], (D_MODEL,), jnp.float32, -s, s)
        wv = jax.random.uniform(ks[5], (D_MODEL, D_MODEL), jnp.float32, -s, s)
        bv = jax.random.uniform(ks[6], (D_MODEL,), jnp.float32, -s, s)
        wo = jax.random.uniform(ks[7], (D_MODEL, D_MODEL), jnp.float32, -s, s)
        bo = jax.random.uniform(ks[8], (D_MODEL,), jnp.float32, -s, s)
        return {'x': x, 'wq': wq, 'bq': bq, 'wk': wk, 'bk': bk, 'wv': wv, 'bv': bv, 'wo': wo, 'bo': bo}
    _L1_attn_in = _L1_attn_setup()

    def _L1_ffn_setup():
        import jax, jax.numpy as jnp
        import numpy as np
        EPS = 1e-08

        def _quantize(w):
            gamma = jnp.mean(jnp.abs(w))
            return jnp.clip(jnp.round(w / (gamma + EPS)), -1.0, 1.0)

        def _bitlinear(x, w):
            return jnp.matmul(x, _quantize(w).T)
        key = jax.random.key(seed)
        k1, k2, k3, k4 = jax.random.split(key, 4)
        d, h = (256, 704)
        x = jax.random.normal(k1, (4, 256, d), dtype=jnp.float32)
        w1 = jax.random.normal(k2, (h, d), dtype=jnp.float32)
        w2 = jax.random.normal(k3, (h, d), dtype=jnp.float32)
        w3 = jax.random.normal(k4, (d, h), dtype=jnp.float32)
        return {'x': x, 'w1': w1, 'w2': w2, 'w3': w3}
    _L1_ffn_in = _L1_ffn_setup()
    _d = {'L0_attn_input': _L0_attn_in['input'], 'L0_attn_W_dt_in': _L0_attn_in['W_dt_in'], 'L0_attn_W_dt_out': _L0_attn_in['W_dt_out'], 'L0_attn_b_dt_out': _L0_attn_in['b_dt_out'], 'L0_attn_W_B': _L0_attn_in['W_B'], 'L0_attn_W_C': _L0_attn_in['W_C'], 'L0_attn_D': _L0_attn_in['D'], 'L0_attn_A_log': _L0_attn_in['A_log'], 'L0_ffn_W_up': _L0_ffn_in['W_up'], 'L0_ffn_W_gate': _L0_ffn_in['W_gate'], 'L0_ffn_W_down': _L0_ffn_in['W_down'], 'L1_attn_wq': _L1_attn_in['wq'], 'L1_attn_bq': _L1_attn_in['bq'], 'L1_attn_wk': _L1_attn_in['wk'], 'L1_attn_bk': _L1_attn_in['bk'], 'L1_attn_wv': _L1_attn_in['wv'], 'L1_attn_bv': _L1_attn_in['bv'], 'L1_attn_wo': _L1_attn_in['wo'], 'L1_attn_bo': _L1_attn_in['bo'], 'L1_ffn_w1': _L1_ffn_in['w1'], 'L1_ffn_w2': _L1_ffn_in['w2'], 'L1_ffn_w3': _L1_ffn_in['w3']}
    _x0 = _d['L0_attn_input']
    _d['L0_attn_input'] = jax.random.normal(jax.random.fold_in(jax.random.key(seed), 1), (4, 1024, 256), dtype=_x0.dtype)
    del _x0
    return _d

def reference(L0_attn_input, L0_attn_W_dt_in, L0_attn_W_dt_out, L0_attn_b_dt_out, L0_attn_W_B, L0_attn_W_C, L0_attn_D, L0_attn_A_log, L0_ffn_W_up, L0_ffn_W_gate, L0_ffn_W_down, L1_attn_wq, L1_attn_bq, L1_attn_wk, L1_attn_bk, L1_attn_wv, L1_attn_bv, L1_attn_wo, L1_attn_bo, L1_ffn_w1, L1_ffn_w2, L1_ffn_w3):

    def _L0_attn_ref(input, W_dt_in, W_dt_out, b_dt_out, W_B, W_C, D, A_log):
        import jax, jax.numpy as jnp
        import numpy as np
        STATE_SIZE = 16
        HIDDEN = 256
        DT_RANK = 64
        BATCH = 2
        SEQ = 256
        A = -jnp.exp(A_log)
        B = jnp.einsum('bsh,nh->bsn', input, W_B)
        C = jnp.einsum('bsh,nh->bsn', input, W_C)
        dt = jnp.einsum('bsh,rh->bsr', input, W_dt_in)
        dt = jnp.einsum('bsr,hr->bsh', dt, W_dt_out) + b_dt_out
        dt = jax.nn.softplus(dt)
        A_disc = jnp.exp(A[None, None] * dt[..., None])
        B_disc = dt[..., None] * B[:, :, None, :]

        def step(x, t):
            a_t, b_t, c_t, u_t = t
            x = a_t * x + b_t * u_t[..., None]
            y = jnp.einsum('bn,bhn->bh', c_t, x) + D * u_t
            return (x, y)
        xs = (jnp.moveaxis(A_disc, 1, 0), jnp.moveaxis(B_disc, 1, 0), jnp.moveaxis(C, 1, 0), jnp.moveaxis(input, 1, 0))
        x0 = jnp.zeros((input.shape[0], D.shape[0], A_log.shape[1]), dtype=input.dtype)
        _, ys = jax.lax.scan(step, x0, xs)
        return jnp.moveaxis(ys, 0, 1)

    def _L0_ffn_ref(x, W_up, W_gate, W_down):
        import jax, jax.numpy as jnp
        import numpy as np
        D_MODEL = 256
        D_EXPERT = 1024
        EPS = 1e-08

        def ternary_quant(w):
            scale = jnp.mean(jnp.abs(w)) + EPS
            q = jnp.clip(jnp.round(w / scale), -1.0, 1.0) * scale
            return w + jax.lax.stop_gradient(q - w)
        wu = ternary_quant(W_up)
        wg = ternary_quant(W_gate)
        wd = ternary_quant(W_down)
        up = jnp.einsum('bsd,ed->bse', x, wu)
        gate = jnp.einsum('bsd,ed->bse', x, wg)
        hidden = jax.nn.silu(up) * gate
        return jnp.einsum('bse,de->bsd', hidden, wd)

    def _L1_attn_ref(x, wq, bq, wk, bk, wv, bv, wo, bo):
        import jax, jax.numpy as jnp
        import numpy as np
        D_MODEL = 256
        NUM_HEADS = 16
        D_K = D_MODEL // NUM_HEADS

        def _heads(t, B, S):
            return t.reshape(B, S, NUM_HEADS, D_K).transpose(0, 2, 1, 3)
        B, S, _ = x.shape
        Q = _heads(x @ wq.T + bq, B, S)
        K = _heads(x @ wk.T + bk, B, S)
        V = _heads(x @ wv.T + bv, B, S)
        Q = jax.nn.elu(Q) + 1.0
        K = jax.nn.elu(K) + 1.0
        KV = jnp.einsum('bhsd,bhse->bhde', K, V)
        QKV = jnp.einsum('bhsd,bhde->bhse', Q, KV)
        K_sum = jnp.sum(K, axis=-2)
        QK_sum = jnp.einsum('bhsd,bhd->bhs', Q, K_sum)
        out = QKV / (QK_sum[..., None] + 1e-08)
        out = out.transpose(0, 2, 1, 3).reshape(B, S, D_MODEL)
        return out @ wo.T + bo

    def _L1_ffn_ref(x, w1, w2, w3):
        import jax, jax.numpy as jnp
        import numpy as np
        EPS = 1e-08

        def _quantize(w):
            gamma = jnp.mean(jnp.abs(w))
            return jnp.clip(jnp.round(w / (gamma + EPS)), -1.0, 1.0)

        def _bitlinear(x, w):
            return jnp.matmul(x, _quantize(w).T)
        x1 = _bitlinear(x, w1)
        x2 = _bitlinear(x, w2)
        hidden = jax.nn.sigmoid(x1) * x2
        return _bitlinear(hidden, w3)
    x = L0_attn_input
    xn = _layernorm(x, axis=-1)
    x = x + _L0_attn_ref(xn, L0_attn_W_dt_in, L0_attn_W_dt_out, L0_attn_b_dt_out, L0_attn_W_B, L0_attn_W_C, L0_attn_D, L0_attn_A_log) + _L0_ffn_ref(xn, L0_ffn_W_up, L0_ffn_W_gate, L0_ffn_W_down)
    xn = _layernorm(x, axis=-1)
    x = x + _L1_attn_ref(xn, L1_attn_wq, L1_attn_bq, L1_attn_wk, L1_attn_bk, L1_attn_wv, L1_attn_bv, L1_attn_wo, L1_attn_bo) + _L1_ffn_ref(xn, L1_ffn_w1, L1_ffn_w2, L1_ffn_w3)
    return x

_drawn_inputs = setup_inputs


def setup_inputs(seed=0):
    import zlib

    import numpy as np

    out = dict(_drawn_inputs(seed))
    spreads = {}
    factors = {'L1_attn_wq': 64.0,
     'L1_attn_bq': 193.351,
     'L1_attn_wk': 64.0,
     'L1_attn_bk': 200.0,
     'L1_attn_wv': 64.0,
     'L1_attn_bv': 64.0,
     'L1_attn_wo': 54.33,
     'L1_attn_bo': 200.0}
    for name, (base, spread) in spreads.items():
        noise = np.random.default_rng([zlib.crc32(name.encode()), seed]).standard_normal(out[name].shape)
        drawn = base * np.exp(spread * noise) if base else spread * noise
        out[name] = jnp.asarray(drawn.astype(out[name].dtype))
    for name, factor in factors.items():
        out[name] = (out[name] * factor).astype(out[name].dtype)
    return out
```

```python
import concourse.bass as bass
from concourse import mybir
from contextlib import ExitStack

P = 128
NBATCH, T, H = 4, 1024, 256
BLK = 512
NJ = T // BLK
NT = T // P
KC = H // P
NS, RANK = 16, 64
CB, NQ, SB = 32, 4, 4
NSB = NS // SB
UNITS = KC * NSB * NQ
F0, F1 = 1024, 704
FT0, FT1 = F0 // P, -(-F1 // P)
F1_LAST = F1 - (FT1 - 1) * P
HEADS, DK = 16, 16
HPC = HEADS // KC
OW = P + HPC
LN_EPS, Q_EPS, DEN_EPS = 1e-5, 1e-8, 1e-8

X_SCALE = 2.0 ** 11
UP_Q = 2.0 ** -12
W2_Q = 2.0 ** -5
W3_Q = 2.0 ** -7

S0, S1 = NJ * FT0, NJ * FT1
SALL = S0 + S1
H_RING = FT0
PROD = 6


def two_layer_kernel(nc, x_tok, x_cm, w_in, w_dt_out, b_dt, d_skip, a_log, w_up, w_gate, w_down,
                     wq, bq, wkv, bkv, wo, bo, w1, w2, w3, ident_in, reduce_in, heads_in, head_of_in, out):
    f32, f16 = mybir.dt.float32, mybir.dt.float16
    ALU, ACT, AX = mybir.AluOpType, mybir.ActivationFunctionType, mybir.AxisListType

    with ExitStack() as ctx:
        def sb(name, shape, dt=f32):
            return ctx.enter_context(nc.sbuf_tensor(name, shape, dt))

        def ps(name, shape):
            return ctx.enter_context(nc.psum_tensor(name, shape, f32))

        def sem(name):
            return ctx.enter_context(nc.semaphore(name))

        q_up = sb("q_up", [P, KC, F0], f16)
        q_gate = sb("q_gate", [P, KC, F0], f16)
        q_down = sb("q_down", [P, FT0, H], f16)
        q_w1 = sb("q_w1", [P, KC, F1], f16)
        q_w2 = sb("q_w2", [P, KC, F1], f16)
        q_w3 = sb("q_w3", [P, FT1, H], f16)
        win_sb = sb("win_sb", [P, KC, RANK + 2 * NS])
        wdt_sb = sb("wdt_sb", [RANK, H])
        wq_sb = sb("wq_sb", [P, KC, H])
        wkv_sb = sb("wkv_sb", [P, KC, 2 * H])
        wo_sb = sb("wo_sb", [P, KC, H])
        bkv_sb = sb("bkv_sb", [P, 2 * H])
        cols = sb("cols", [P, 4, KC])
        a_neg = sb("a_neg", [P, KC * NQ * NSB])
        ident = sb("ident", [P, P])
        reduce_w = sb("reduce_w", [P, CB])
        diag_d = sb("diag_d", [P, KC, P])
        heads = sb("heads", [P, P])
        head_of = sb("head_of", [P, HPC])
        ones = sb("ones", [P, P])
        neg_half = sb("neg_half", [P, NT])
        eps = sb("eps", [P, NT])
        spare = sb("spare", [P, 1])
        scale_sb = sb("scale_sb", [P, 5, 6])
        sdown = sb("sdown", [P, 3])

        xtok = sb("xtok", [P, NT, H])
        xt = sb("xt", [P, KC, T])
        xn = sb("xn", [P, KC, T])
        xh = sb("xh", [P, KC, T], f16)
        xl = sb("xl", [P, KC, T], f16)
        stats = sb("stats", [P, NT, 6])
        mv = sb("mv", [P, NT, 2])
        rstd = sb("rstd", [P, 2, NT])
        lbc = sb("lbc", [RANK + 2 * NS, T])
        dt_sb = sb("dt_sb", [P, KC, T])
        dtu = sb("dtu", [P, KC, T])
        bc = sb("bc", [P, 2, NSB, T])
        dtb = sb("dtb", [P, 2, NQ, T])
        a_ring = sb("a_ring", [P, 2, T])
        b_ring = sb("b_ring", [P, 2, T])
        prod = sb("prod", [P, PROD, T])
        th = sb("th", [P, BLK])
        t1 = sb("t1", [P, BLK])
        hid0 = sb("hid0", [P, H_RING, 2, BLK], f16)
        x2tok = dtb[:, 0, 0:2, :].rearrange("p a (t h) -> p (a t) h", h=H)
        qf, ot = dt_sb, dtu
        q_min = dtb[:, 0, 2, :].rearrange("p (r t) -> p r t", r=2)
        k_all = dtb[:, 0, 3, :].rearrange("p (w r t) -> p w r t", w=2, r=2)
        kf = dtb[:, 1, 0, 0:512].rearrange("p (r t) -> p r t", r=2)
        otok = dtb[:, 1, 0, 512:1024].rearrange("p (r t) -> p r t", r=2)
        den = dtb[:, 1, 1, 0:64].rearrange("p (r w h) -> p r w h", r=2, w=2)
        ksum = dtb[:, 1, 1, 64:66]
        vx = sb("vx", [P, 2, KC, P + 1])
        kvx = sb("kvx", [P, KC, OW])
        hid1 = bc[:, :, :, :].rearrange("p w n t -> p (w n t)").bitcast(f16)[:, 0:S1 * 2 * BLK]\
            .rearrange("p (s w t) -> p s w t", s=S1, w=2)
        raw0 = prod[:, :, :].rearrange("p r t -> p (r t)")[:, 0:3 * KC * F0].rearrange("p (w n) -> p w n", w=3)
        RAW1 = FT1 * H
        raw1 = bc[:, :, :, :].rearrange("p w n t -> p (w n t)")[:, 0:3 * RAW1].rearrange("p (w n) -> p w n", w=3)
        junk = dtb[:, 0, 0:2, :].rearrange("p a t -> p (a t)")
        cmp_lo = dtb[:, 1, 0, :].bitcast(f16)
        cmp_hi = dtb[:, 1, 1, :].bitcast(f16)

        ug = ps("ug", [P, 2, BLK])
        acc = ps("acc", [P, 2, BLK])
        xs = ps("xs", [P, T])
        y = ps("y", [P, 2, BLK])

        w_small = sem("w_small"); w_raw0 = sem("w_raw0"); w_raw1 = sem("w_raw1"); w_attn = sem("w_attn")
        raw_tail = sem("raw_tail"); const_set = sem("const_set"); abs_done = sem("abs_done")
        sums_ps = sem("sums_ps"); setup_dve = sem("setup_dve"); quant = sem("quant"); aneg_done = sem("aneg_done")
        xtok_in = sem("xtok_in"); xt_in = sem("xt_in")
        ln_stats = sem("ln_stats")
        rstd_done = sem("rstd_done")
        xn_tok = sem("xn_tok")
        xnt_ps = sem("xnt_ps")
        xh_done = sem("xh_done")
        xl_done = sem("xl_done")
        low_ps = sem("low_ps")
        low_sb = sem("low_sb")
        pre_ps = sem("pre_ps")
        pre_free = sem("pre_free")
        sp_parts = sem("sp_parts")
        dt_done = sem("dt_done")
        bc_dram = sem("bc_dram")
        bc_in = [sem(f"bc_in{n}") for n in range(NSB)]
        dtb_in = [sem(f"dtb_in{n}") for n in range(NQ)]
        a_done = sem("a_done"); b_done = sem("b_done"); scan_done = sem("scan_done"); prod_done = sem("prod_done")
        red_done = sem("red_done")
        y_free = sem("y_free")
        u_ps = sem("u_ps"); g_ps = sem("g_ps"); th_done = sem("th_done"); u_free = sem("u_free")
        r_done = sem("r_done"); hi_done = sem("hi_done"); lo_done = sem("lo_done")
        t1_done = sem("t1_done")
        down_ps = sem("down_ps")
        down_free = sem("down_free")
        x2_ps = sem("x2_ps"); x2_tok = sem("x2_tok")
        q_ps = sem("q_ps"); qm_done = sem("qm_done"); qe_done = sem("qe_done"); qf_done = sem("qf_done")
        kv_ps = sem("kv_ps"); kv_sb = sem("kv_sb"); km_done = sem("km_done"); ke_done = sem("ke_done")
        kf_done = sem("kf_done"); kv_acc = sem("kv_acc")
        kvx_done = sem("kvx_done")
        o_ps = sem("o_ps"); otok_done = sem("otok_done")
        ot_ps = sem("ot_ps"); ot_done = sem("ot_done")
        y2_ps = sem("y2_ps"); out_done = sem("out_done")
        out_dram = sem("out_dram")
        act_self = sem("act_self"); dve_self = sem("dve_self"); pool_self = sem("pool_self")
        quant_self = sem("quant_self"); ksum_done = sem("ksum_done"); den_done = sem("den_done")

        scratch = nc.dram_tensor("bc_scratch", (2 * NS, T), f32, kind="Internal").ap()
        block = ctx.enter_context(nc.Block())



        @block.sync
        def _(sp):
            sp.dma_start(xtok[:, :, :], x_tok[0].rearrange("(t p) h -> p t h", p=P)).then_inc(xtok_in, 16)
            for dst, src in ((ident[:, :], ident_in), (reduce_w[:, :], reduce_in), (heads[:, :], heads_in),
                             (head_of[:, :], head_of_in), (a_neg[:, :], a_log),
                             (win_sb[:, :, :], w_in.rearrange("(k p) m -> p k m", p=P)), (wdt_sb[:, :], w_dt_out),
                             (cols[:, 0, :], b_dt.rearrange("(k p) -> p k", p=P)),
                             (cols[:, 1, :], d_skip.rearrange("(k p) -> p k", p=P)),
                             (cols[:, 2, :], bq.rearrange("(k p) -> p k", p=P)),
                             (cols[:, 3, :], bo.rearrange("(k p) -> p k", p=P))):
                with nc.allow_non_contiguous_dma(reason="a few short columns"):
                    sp.dma_start(dst, src).then_inc(w_small, 16)
            for n, w in enumerate((w_up, w_gate, w_down)):
                sp.dma_start(raw0[:, n, :].rearrange("p (k m) -> p k m", k=w.shape[0] // P),
                             w.rearrange("(k p) m -> p k m", p=P)).then_inc(w_raw0, 16)
            for n, w in enumerate((w1, w2)):
                sp.dma_start(raw1[:, n, 0:KC * F1].rearrange("p (k m) -> p k m", k=KC),
                             w.rearrange("(k p) m -> p k m", p=P)).then_inc(w_raw1, 16)
            full = (FT1 - 1) * P
            sp.dma_start(raw1[:, 2, 0:(FT1 - 1) * H].rearrange("p (k m) -> p k m", k=FT1 - 1),
                         w3[0:full, :].rearrange("(k p) m -> p k m", p=P)).then_inc(w_raw1, 16)
            sp.dma_start(raw1[0:F1_LAST, 2, (FT1 - 1) * H:FT1 * H], w3[full:F1, :]).then_inc(w_raw1, 16)
            for dst, src in ((wq_sb, wq), (wkv_sb, wkv), (wo_sb, wo)):
                sp.dma_start(dst[:, :, :], src.rearrange("(k p) m -> p k m", p=P)).then_inc(w_attn, 16)
            sp.dma_start(bkv_sb[:, :], bkv.rearrange("(a n) -> a n", a=1).to_broadcast([P, 2 * H])).then_inc(w_attn, 16)

            def batch(i, first):
                def at(per_batch, n):
                    return n if first else sp.snap(i * per_batch + n)

                transposed, stored, low_ready = at(8, -4), at(64, 0), at(2, 2)
                summed, in_dram = at(4, 0), at(16, 16)
                steps = [at(2, c + 1) for c in range(KC)]
                last_units = [at(UNITS, NSB * NQ - NQ + q + 1) for q in range(NQ)]
                if not first:
                    sp.wait_ge(xnt_ps, transposed)
                    sp.dma_start(xtok[:, :, :], x_tok[i].rearrange("(t p) h -> p t h", p=P)).then_inc(xtok_in, 16)
                    sp.wait_ge(out_dram, stored)
                sp.dma_start(xt[:, :, :], x_cm[i].rearrange("(k p) t -> p k t", p=P)).then_inc(xt_in, 16)
                if first:
                    sp.wait_ge(quant, 6)
                else:
                    sp.wait_ge(y2_ps, summed)
                sp.wait_ge(low_sb, low_ready)
                sp.dma_start(scratch, lbc[RANK:RANK + 2 * NS, :]).then_inc(bc_dram, 16)
                sp.wait_ge(bc_dram, in_dram)
                for nb in range(NSB):
                    for w in range(2):
                        row = w * NS + nb * SB
                        sp.dma_start(bc[:, w, nb, :],
                                     scratch[row:row + SB, :].unsqueeze(0).to_broadcast([CB, SB, T]))\
                          .then_inc(bc_in[nb], 16)
                for c in range(KC):
                    sp.wait_ge(dt_done, steps[c])
                    for q in range(NQ):
                        if c:
                            sp.wait_ge(a_done, last_units[q])
                            sp.wait_ge(b_done, last_units[q])
                        for w, src in enumerate((dt_sb, dtu)):
                            sp.dma_start(dtb[:, w, q, :],
                                         src[q * CB:(q + 1) * CB, c, :].unsqueeze(1).to_broadcast([CB, SB, T]))\
                              .then_inc(dtb_in[q], 16)

            batch(0, True)
            with sp.Fori(1, NBATCH) as i:
                batch(i, False)
            sp.wait_ge(out_dram, NBATCH * 64)
            sp.wait_ge(bc_dram, NBATCH * 16)

        @block.scalar
        def _(act):
            act.wait_ge(w_small, 11 * 16)
            nc.scalar.activation(a_neg[:, :], a_neg[:, :], ACT.Exp).then_inc(aneg_done, 1)

            def magnitudes(layer):
                if layer == 0:
                    act.wait_ge(w_raw0, 3 * 16)
                else:
                    act.wait_ge(w_raw1, 4 * 16)
                    act.wait_ge(raw_tail, 1)
                for n in range(3):
                    raw = (raw0, raw1)[layer]
                    m = (KC * F0, KC * F0, FT0 * H, KC * F1, KC * F1, RAW1)[3 * layer + n]
                    nc.scalar.activation(junk[:, 0:m], raw[:, n, 0:m], ACT.Abs,
                                         accum_out=scale_sb[:, 0, 3 * layer + n:3 * layer + n + 1])\
                        .then_inc(abs_done, 1)
                    act.wait_ge(abs_done, 3 * layer + n + 1)

            def xn_parts(i, l):
                for j in range(NJ):
                    for c in range(KC):
                        act.wait_ge(xnt_ps, i * 8 + l * 4 + j * 2 + c + 1)
                        nc.scalar.activation(xn[:, c, j * BLK:(j + 1) * BLK], ug[:, c, :], ACT.Copy)
                        nc.scalar.activation(xh[:, c, j * BLK:(j + 1) * BLK], ug[:, c, :], ACT.Copy,
                                             scale=X_SCALE).then_inc(xh_done, 1)

            def tanh(i, s, scale, frees_u):
                act.wait_ge(u_ps, i * SALL + s + 1)
                if frees_u:
                    if s == S0:
                        act.wait_ge(t1_done, i * S0 + S0)
                    else:
                        act.wait_ge(r_done, i * SALL + s)
                    rows = F1_LAST if (s - S0) % FT1 == FT1 - 1 else P
                    nc.scalar.activation(th[0:rows, :], ug[0:rows, 0, :], ACT.Tanh, scale=scale).then_inc(th_done, 1)
                else:
                    if s:
                        act.wait_ge(t1_done, i * S0 + s)
                    nc.scalar.activation(th[:, :], ug[:, 0, :], ACT.Tanh, scale=scale).then_inc(th_done, 1)

            def high(i, s, dst, rows=P):
                act.wait_ge(r_done, i * SALL + s + 1)
                nc.scalar.activation(dst[0:rows, :], ug[0:rows, 1, :], ACT.Copy).then_inc(hi_done, 1)

            def batch(i, first):
                xn_parts(i, 0)
                for j in range(NJ):
                    act.wait_ge(low_ps, i * 2 + j + 1)
                    nc.scalar.activation(lbc[:, j * BLK:(j + 1) * BLK], acc[0:RANK + 2 * NS, j, :],
                                         ACT.Copy).then_inc(low_sb, 1)
                if first:
                    magnitudes(0)
                pre = (ug[:, :, :].rearrange("p a t -> p (a t)"), xs[:, :])
                own = i * 4
                for c in range(KC):
                    act.wait_ge(pre_ps, i * 2 + c + 1)
                    nc.scalar.activation(dt_sb[:, c, :], pre[c], ACT.Abs, bias=cols[:, 0, c:c + 1])\
                        .then_inc(act_self, 1)
                    nc.scalar.activation(dtu[:, c, :], pre[c], ACT.Relu, bias=cols[:, 0, c:c + 1])\
                        .then_inc(pre_free, 1)
                for c in range(KC):
                    act.wait_ge(act_self, own + c + 1)
                    nc.scalar.activation(dt_sb[:, c, :], dt_sb[:, c, :], ACT.Exp, scale=-1.0).then_inc(act_self, 1)
                for c in range(KC):
                    act.wait_ge(act_self, own + KC + c + 1)
                    nc.scalar.activation(dt_sb[:, c, :], dt_sb[:, c, :], ACT.Ln, bias=1.0).then_inc(sp_parts, 1)
                if first:
                    magnitudes(1)
                    act.wait_ge(setup_dve, 2)

                def decay(u):
                    c, q = u // 16, u % 4
                    act.wait_ge(dtb_in[q], i * 64 + c * 32 + 32)
                    if u >= 2:
                        act.wait_ge(scan_done, i * UNITS + u - 1)
                    k = (c * NQ + q) * NSB + u % 16 // 4
                    nc.scalar.activation(a_ring[:, u % 2, :], dtb[:, 0, q, :], ACT.Exp,
                                         scale=a_neg[:, k:k + 1]).then_inc(a_done, 1)

                def gated0(s):
                    tanh(i, s, scale_sb[:, 2, 0:1], False)

                def high0(s):
                    if s >= H_RING:
                        act.wait_ge(down_ps, i * 4 + 2)
                    elif not first:
                        act.wait_ge(down_ps, i * 4)
                    high(i, s, hid0[:, s % H_RING, 0, :])

                for g in range(8):
                    decay(4 * g)
                    gated0(2 * g)
                    decay(4 * g + 1)
                    high0(2 * g)
                    decay(4 * g + 2)
                    gated0(2 * g + 1)
                    decay(4 * g + 3)
                    high0(2 * g + 1)

                for p in range(4):
                    act.wait_ge(x2_ps, i * 4 + p + 1)
                    nc.scalar.activation(x2tok[:, 2 * p:2 * p + 2, :],
                                         ug[:, p % 2, :].rearrange("p (t h) -> p t h", t=2),
                                         ACT.Copy).then_inc(x2_tok, 1)
                xn_parts(i, 1)

                def gated1(s):
                    tanh(i, s, 1.0, True)

                def high1(s):
                    rows = F1_LAST if (s - S0) % FT1 == FT1 - 1 else P
                    high(i, s, hid1[:, s - S0, 0, :], rows)

                def q_feature(n):
                    c, j = n % 2, n // 2
                    act.wait_ge(qm_done, i * 4 + n + 1)
                    nc.scalar.activation(qf[:, c, j * BLK:(j + 1) * BLK], xs[:, n % 2 * BLK:(n % 2 + 1) * BLK],
                                         ACT.Relu, bias=cols[:, 2, c:c + 1])
                    nc.scalar.activation(q_min[:, n % 2, :], q_min[:, n % 2, :], ACT.Exp).then_inc(qe_done, 1)

                def k_feature(t):
                    act.wait_ge(km_done, i * 8 + t + 1)
                    nc.scalar.activation(k_all[:, 1, t % 2, :], k_all[:, 1, t % 2, :], ACT.Exp).then_inc(ke_done, 1)

                for s in range(S1):
                    gated1(S0 + s)
                    if s < 4:
                        q_feature(s)
                    else:
                        k_feature(s - 4)
                    high1(S0 + s)
                for j in range(NJ):
                    act.wait_ge(ot_ps, i * 2 + j + 1)
                    for c in range(KC):
                        last = nc.scalar.activation(ot[:, c, j * BLK:(j + 1) * BLK], acc[:, c, :], ACT.Copy)
                    last.then_inc(ot_done, 1)
                for j in range(NJ):
                    for c in range(KC):
                        act.wait_ge(out_done, i * 4 + j * 2 + c + 1)
                        act.dma_start(out[i, c * P:(c + 1) * P, j * BLK:(j + 1) * BLK],
                                      xt[:, c, j * BLK:(j + 1) * BLK]).then_inc(out_dram, 16)

            batch(0, True)
            with act.Fori(1, NBATCH) as i:
                batch(i, False)

        @block.gpsimd
        def _(pool):
            nc.gpsimd.memset(raw1[F1_LAST:P, 2, (FT1 - 1) * H:FT1 * H], 0.0).then_inc(raw_tail, 1)
            pool.wait_ge(raw_tail, 1)
            nc.gpsimd.memset(neg_half[:, :], -0.5)
            nc.gpsimd.memset(eps[:, :], LN_EPS)
            nc.gpsimd.memset(vx[:, :, :, P:P + 1], 1.0)
            nc.gpsimd.memset(ones[:, :], 1.0).then_inc(const_set, 1)
            pool.wait_ge(const_set, 1)

            def rstd_of(i, l):
                pool.wait_ge(ln_stats, i * 2 + l + 1)
                nc.gpsimd.tensor_tensor(out=rstd[:, 0, :], in0=mv[:, :, 1], in1=eps[:, :], op=ALU.add).then_inc(pool_self, 1)
                pool.wait_ge(pool_self, i * (2 + KC) + (l * (1 + KC)) + 1)
                nc.gpsimd.tensor_tensor(out=rstd[:, 1, :], in0=rstd[:, 0, :], in1=neg_half[:, :], op=ALU.pow)\
                    .then_inc(rstd_done, 1)

            def batch(i, first):
                rstd_of(i, 0)
                for c in range(KC):
                    pool.wait_ge(sp_parts, i * 2 + c + 1)
                    nc.gpsimd.tensor_tensor(out=dt_sb[:, c, :], in0=dt_sb[:, c, :], in1=dtu[:, c, :], op=ALU.add)\
                        .then_inc(pool_self, 1)
                    pool.wait_ge(pool_self, i * (2 + KC) + 2 + c)
                    nc.gpsimd.tensor_tensor(out=dtu[:, c, :], in0=dt_sb[:, c, :], in1=xn[:, c, :], op=ALU.mult)\
                        .then_inc(dt_done, 1)
                for u in range(UNITS):
                    c, nb, q = u // 16, u % 16 // 4, u % 4
                    pool.wait_ge(dtb_in[q], i * 64 + c * 32 + 32)
                    pool.wait_ge(bc_in[nb], i * 32 + 32)
                    if u >= 2:
                        pool.wait_ge(scan_done, i * UNITS + u - 1)
                    nc.gpsimd.tensor_tensor(out=b_ring[:, u % 2, :], in0=dtb[:, 1, q, :], in1=bc[:, 0, nb, :],
                                            op=ALU.mult).then_inc(b_done, 1)
                rstd_of(i, 1)
                for n in range(4):
                    c, j = n % 2, n // 2
                    pool.wait_ge(qe_done, i * 4 + n + 1)
                    part = qf[:, c, j * BLK:(j + 1) * BLK]
                    nc.gpsimd.tensor_tensor(out=part, in0=part, in1=q_min[:, n % 2, :], op=ALU.add)\
                        .then_inc(qf_done, 1)

            batch(0, True)
            with pool.Fori(1, NBATCH) as i:
                batch(i, False)

        @block.vector
        def _(dve):
            def norm(i, l, tok):
                own = (i * 2 + l) * 1
                for t in range(NT):
                    last = nc.vector.bn_stats(stats[:, t, :], tok[:, t, :])
                last.then_inc(dve_self, 1)
                dve.wait_ge(dve_self, own + 1)
                nc.vector.memset(spare[:, :], 0.0)
                for t in range(NT):
                    last = nc.vector.bn_aggr(mv[:, t, :], stats[:, t, :])
                last.then_inc(ln_stats, 1)
                dve.wait_ge(rstd_done, i * 2 + l + 1)
                for t in range(NT):
                    nc.vector.tensor_scalar(tok[:, t, :], tok[:, t, :], mv[:, t, 0:1], rstd[:, 1, t:t + 1],
                                            ALU.subtract, ALU.mult).then_inc(xn_tok, 1)

            def low_part(i, l):
                for j in range(NJ):
                    for c in range(KC):
                        cut = slice(j * BLK, (j + 1) * BLK)
                        dve.wait_ge(xh_done, i * 8 + l * 4 + j * 2 + c + 1)
                        nc.vector.scalar_tensor_tensor(out=xl[:, c, cut], in0=ug[:, c, :], scalar=X_SCALE,
                                                       in1=xh[:, c, cut], op0=ALU.mult, op1=ALU.subtract)\
                            .then_inc(xl_done, 1)

            def setup():
                dve.wait_ge(w_small, 11 * 16)
                for c in range(KC):
                    nc.vector.tensor_scalar(diag_d[:, c, :], ident[:, :], cols[:, 1, c:c + 1], None, ALU.mult)
                dve.wait_ge(aneg_done, 1)
                nc.vector.tensor_scalar(a_neg[:, :], a_neg[:, :], -1.0, None, ALU.mult).then_inc(setup_dve, 1)

            chain = [0]

            def link(ins):
                chain[0] += 1
                ins.then_inc(quant_self, 1)
                dve.wait_ge(quant_self, chain[0])

            def thresholds():
                dve.wait_ge(sums_ps, 1)
                link(nc.vector.tensor_scalar(scale_sb[:, 1, 0:3], y[:, 0, 0:3], 1.0 / (F0 * H), None, ALU.mult))
                link(nc.vector.tensor_scalar(scale_sb[:, 1, 3:6], y[:, 0, 3:6], 1.0 / (F1 * H), None, ALU.mult))
                link(nc.vector.tensor_scalar(scale_sb[:, 2, :], scale_sb[:, 1, :], Q_EPS, None, ALU.add))
                nc.vector.tensor_scalar(scale_sb[:, 3, :], scale_sb[:, 2, :], 0.5, None, ALU.mult)
                link(nc.vector.tensor_scalar(scale_sb[:, 4, :], scale_sb[:, 2, :], -0.5, None, ALU.mult))
                link(nc.vector.tensor_tensor(out=sdown[:, 0:1], in0=scale_sb[:, 2, 0:1], in1=scale_sb[:, 2, 1:2],
                                             op=ALU.mult))
                nc.vector.scalar_tensor_tensor(out=sdown[:, 1:2], in0=sdown[:, 0:1], scalar=2.0,
                                               in1=scale_sb[:, 2, 2:3], op0=ALU.mult, op1=ALU.mult)\
                    .then_inc(setup_dve, 1)

            def quantise(n, dst, src, size, q):
                nc.vector.tensor_scalar(cmp_lo[:, 0:size], src, scale_sb[:, 4, n:n + 1], q, ALU.is_lt, ALU.mult)
                link(nc.vector.tensor_scalar(cmp_hi[:, 0:size], src, scale_sb[:, 3, n:n + 1], q, ALU.is_gt, ALU.mult))
                nc.vector.tensor_tensor(out=dst, in0=cmp_hi[:, 0:size], in1=cmp_lo[:, 0:size], op=ALU.subtract)\
                    .then_inc(quant, 1)
                dve.wait_ge(quant, n + 1)

            def flat(w):
                return w[:, :, :].rearrange("p k m -> p (k m)")

            def batch(i, first):
                dve.wait_ge(xtok_in, i * 16 + 16)
                norm(i, 0, xtok)
                low_part(i, 0)
                if first:
                    setup()
                    thresholds()
                    quantise(0, flat(q_up), raw0[:, 0, :], KC * F0, UP_Q)
                    quantise(1, flat(q_gate), raw0[:, 1, :], KC * F0, UP_Q)
                    quantise(2, flat(q_down), raw0[:, 2, :], KC * F0, 1.0)
                    quantise(3, flat(q_w1), raw1[:, 0, 0:KC * F1], KC * F1, UP_Q)
                    quantise(4, flat(q_w2), raw1[:, 1, 0:KC * F1], KC * F1, W2_Q)
                    quantise(5, flat(q_w3), raw1[:, 2, :], RAW1, W3_Q)

                def unit(u):
                    nb = u % 16 // 4
                    dve.wait_ge(a_done, i * UNITS + u + 1)
                    dve.wait_ge(b_done, i * UNITS + u + 1)
                    if u or not first:
                        dve.wait_ge(prod_done, i * UNITS + u)
                    nc.vector.tensor_tensor_scan(out=xs[:, :], data0=a_ring[:, u % 2, :], data1=b_ring[:, u % 2, :],
                                                 initial=0.0, op0=ALU.mult, op1=ALU.add).then_inc(scan_done, 1)
                    if u >= PROD:
                        dve.wait_ge(red_done, i * 8 + (u - PROD) // 4 + 1)
                    dve.wait_ge(bc_in[nb], i * 32 + 32)
                    dve.wait_ge(scan_done, i * UNITS + u + 1)
                    nc.vector.tensor_tensor(out=prod[:, u % PROD, :], in0=xs[:, :], in1=bc[:, 1, nb, :],
                                            op=ALU.mult).then_inc(prod_done, 1)

                def gate0(s):
                    dve.wait_ge(th_done, i * SALL + s + 1)
                    nc.vector.scalar_tensor_tensor(out=t1[:, :], in0=th[:, :], scalar=1.0, in1=ug[:, 0, :],
                                                   op0=ALU.add, op1=ALU.mult).then_inc(t1_done, 1)
                    dve.wait_ge(g_ps, i * SALL + s + 1)
                    dve.wait_ge(t1_done, i * S0 + s + 1)
                    nc.vector.tensor_tensor(out=ug[:, 1, :], in0=t1[:, :], in1=ug[:, 1, :], op=ALU.mult)\
                        .then_inc(r_done, 1)

                def low0(s):
                    dve.wait_ge(hi_done, i * SALL + s + 1)
                    nc.vector.tensor_tensor(out=hid0[:, s % H_RING, 1, :], in0=ug[:, 1, :],
                                            in1=hid0[:, s % H_RING, 0, :], op=ALU.subtract).then_inc(lo_done, 1)

                def add_down(j, c):
                    dve.wait_ge(down_ps, i * 4 + j * 2 + c + 1)
                    part = xt[:, c, j * BLK:(j + 1) * BLK]
                    nc.vector.scalar_tensor_tensor(out=part, in0=acc[:, c, :], scalar=sdown[:, 1:2], in1=part,
                                                   op0=ALU.mult, op1=ALU.add).then_inc(down_free, 1)

                def add_y(c):
                    dve.wait_ge(red_done, i * 8 + c * 4 + 4)
                    nc.vector.tensor_tensor(out=xt[:, c, :], in0=y[:, :, :].rearrange("p a t -> p (a t)"),
                                            in1=xt[:, c, :], op=ALU.add).then_inc(y_free, 1)

                dve.wait_ge(xt_in, i * 16 + 16)
                for g in range(8):
                    unit(4 * g)
                    if g == 4:
                        add_y(0)
                        dve.wait_ge(y_free, i * 2 + 1)
                    gate0(2 * g)
                    unit(4 * g + 1)
                    low0(2 * g)
                    if g == 5:
                        for c in range(KC):
                            add_down(0, c)
                    unit(4 * g + 2)
                    gate0(2 * g + 1)
                    unit(4 * g + 3)
                    low0(2 * g + 1)
                add_y(1)
                dve.wait_ge(y_free, i * 2 + 2)
                dve.wait_ge(down_free, i * 4 + 2)
                for c in range(KC):
                    add_down(1, c)

                dve.wait_ge(x2_tok, i * 4 + 4)
                norm(i, 1, x2tok)
                low_part(i, 1)

                def gate1(s):
                    rows = F1_LAST if (s - S0) % FT1 == FT1 - 1 else P
                    dve.wait_ge(th_done, i * SALL + s + 1)
                    dve.wait_ge(g_ps, i * SALL + s + 1)
                    nc.vector.scalar_tensor_tensor(out=ug[0:rows, 1, :], in0=th[0:rows, :], scalar=1.0,
                                                   in1=ug[0:rows, 1, :], op0=ALU.add, op1=ALU.mult)\
                        .then_inc(r_done, 1)

                def low1(s):
                    rows = F1_LAST if (s - S0) % FT1 == FT1 - 1 else P
                    dve.wait_ge(hi_done, i * SALL + s + 1)
                    nc.vector.tensor_tensor(out=hid1[0:rows, s - S0, 1, :], in0=ug[0:rows, 1, :],
                                            in1=hid1[0:rows, s - S0, 0, :], op=ALU.subtract).then_inc(lo_done, 1)

                def q_minimum(n):
                    c = n % 2
                    dve.wait_ge(q_ps, i * 4 + n + 1)
                    if n >= 2:
                        dve.wait_ge(qf_done, i * 4 + n - 1)
                    nc.vector.tensor_scalar(q_min[:, n % 2, :], xs[:, n % 2 * BLK:(n % 2 + 1) * BLK],
                                            cols[:, 2, c:c + 1], 0.0, ALU.add, ALU.min).then_inc(qm_done, 1)

                def kv_bias(t):
                    dve.wait_ge(kv_ps, i * 8 + t + 1)
                    bank = xs[:, t % 2 * BLK:(t % 2 + 1) * BLK]
                    if t >= 2:
                        dve.wait_ge(kv_acc, i * 8 + t - 1)
                        dve.wait_ge(kf_done, i * 8 + t - 1)
                    nc.vector.tensor_tensor(out=vx[:, t % 2, :, 0:P],
                                            in0=bank[:, H:2 * H].rearrange("p (c m) -> p c m", c=KC),
                                            in1=bkv_sb[:, H:2 * H].rearrange("p (c m) -> p c m", c=KC), op=ALU.add)
                    nc.vector.tensor_tensor(out=k_all[:, 0, t % 2, :], in0=bank[:, 0:H], in1=bkv_sb[:, 0:H],
                                            op=ALU.add).then_inc(kv_sb, 1)
                    dve.wait_ge(kv_sb, i * 8 + t + 1)
                    nc.vector.tensor_scalar(k_all[:, 1, t % 2, :], k_all[:, 0, t % 2, :], 0.0, None, ALU.min)\
                        .then_inc(km_done, 1)

                def k_feature(t):
                    dve.wait_ge(ke_done, i * 8 + t + 1)
                    if t >= 2:
                        dve.wait_ge(kv_acc, i * 8 + t - 1)
                    nc.vector.scalar_tensor_tensor(out=kf[:, t % 2, :], in0=k_all[:, 0, t % 2, :], scalar=0.0,
                                                   in1=k_all[:, 1, t % 2, :], op0=ALU.max, op1=ALU.add)\
                        .then_inc(kf_done, 1)

                for s in range(S1):
                    gate1(S0 + s)
                    if s < 4:
                        q_minimum(s)
                    else:
                        kv_bias(s - 4)
                    low1(S0 + s)
                    if s >= 4:
                        k_feature(s - 4)
                dve.wait_ge(kv_acc, i * 8 + 8)
                for c in range(KC):
                    nc.vector.tensor_tensor(out=kvx[:, c, 0:P], in0=acc[:, c, 0:P], in1=heads[:, :], op=ALU.mult)
                    last = nc.vector.tensor_copy(ksum[:, c:c + 1], acc[:, c, P:P + 1])
                last.then_inc(ksum_done, 1)
                dve.wait_ge(ksum_done, i + 1)
                for c in range(KC):
                    last = nc.vector.tensor_scalar(kvx[:, c, P:OW], head_of[:, :], ksum[:, c:c + 1], None, ALU.mult)
                last.then_inc(kvx_done, 1)
                for t in range(NT):
                    r = t % 2
                    dve.wait_ge(o_ps, i * 8 + t + 1)
                    bank = y[:, r, 0:KC * OW].rearrange("p (c w) -> p c w", c=KC)
                    nc.vector.tensor_scalar(den[:, r, 0, :].rearrange("p (c h) -> p c h", c=KC), bank[:, :, P:OW],
                                            DEN_EPS, None, ALU.add).then_inc(den_done, 1)
                    dve.wait_ge(den_done, i * 16 + 2 * t + 1)
                    nc.vector.reciprocal(den[:, r, 1, :], den[:, r, 0, :]).then_inc(den_done, 1)
                    dve.wait_ge(den_done, i * 16 + 2 * t + 2)
                    for c in range(KC):
                        last = nc.vector.tensor_tensor(
                            out=otok[:, r, c * P:(c + 1) * P].rearrange("p (h e) -> p h e", e=DK),
                            in0=bank[:, c, 0:P].rearrange("p (h e) -> p h e", e=DK),
                            in1=den[:, r, 1, c * HPC:(c + 1) * HPC].unsqueeze(2).to_broadcast([P, HPC, DK]),
                            op=ALU.mult)
                    last.then_inc(otok_done, 1)
                for j in range(NJ):
                    for c in range(KC):
                        dve.wait_ge(y2_ps, i * 4 + j * 2 + c + 1)
                        part = xt[:, c, j * BLK:(j + 1) * BLK]
                        nc.vector.scalar_tensor_tensor(out=part, in0=acc[:, c, :], scalar=cols[:, 3, c:c + 1],
                                                       in1=part, op0=ALU.add, op1=ALU.add).then_inc(out_done, 1)

            batch(0, True)
            with dve.Fori(1, NBATCH) as i:
                batch(i, False)

        @block.tensor
        def _(pe):
            mm = nc.tensor.matmul

            def to_channels(i, l, tok):
                for j in range(NJ):
                    pe.wait_ge(xn_tok, i * 16 + l * 8 + j * 4 + 4)
                    for c in range(KC):
                        if j:
                            pe.wait_ge(xl_done, i * 8 + l * 4 + c + 1)
                        for t in range(4):
                            last = nc.tensor.transpose(ug[:, c, t * P:(t + 1) * P],
                                                       tok[:, 4 * j + t, c * P:(c + 1) * P], ident[:, :])
                        last.then_inc(xnt_ps, 1)

            def wide(i, s, bank, w, f, m, j, done):
                cut = slice(j * BLK, (j + 1) * BLK)
                n = 0
                for k in range(KC):
                    for part in (xh, xl):
                        last = mm(ug[0:m, bank, :], w[:, k, f * P:f * P + m], part[:, k, cut],
                                  start=(n == 0), stop=(n == 2 * KC - 1))
                        n += 1
                last.then_inc(done, 1)

            def batch(i, first):
                if first:
                    pe.wait_ge(w_small, 11 * 16)
                else:
                    pe.wait_ge(lo_done, i * SALL)
                to_channels(i, 0, xtok)
                pe.wait_ge(xl_done, i * 8 + 4)
                for j in range(NJ):
                    if not first and j == 0:
                        pe.wait_ge(out_done, i * 4)
                    for k in range(KC):
                        last = mm(acc[0:RANK + 2 * NS, j, :], win_sb[:, k, :], xn[:, k, j * BLK:(j + 1) * BLK],
                                  start=(k == 0), stop=(k == KC - 1))
                    last.then_inc(low_ps, 1)
                if not first:
                    pe.wait_ge(kv_sb, i * 8)
                pe.wait_ge(low_sb, i * 2 + 2)
                for c in range(KC):
                    for j in range(NJ):
                        dst = (ug[:, j, :], xs[:, j * BLK:(j + 1) * BLK])[c]
                        last = mm(dst, wdt_sb[:, c * P:(c + 1) * P], lbc[0:RANK, j * BLK:(j + 1) * BLK],
                                  start=True, stop=True)
                    last.then_inc(pre_ps, 1)
                if first:
                    pe.wait_ge(const_set, 1)
                    pe.wait_ge(abs_done, 6)
                    mm(y[:, 0, 0:6], ones[:, :], scale_sb[:, 0, :], start=True, stop=True).then_inc(sums_ps, 1)
                    pe.wait_ge(quant, 3)

                def gated0(s):
                    j, f = s // FT0, s % FT0
                    if s:
                        pe.wait_ge(t1_done, i * S0 + s)
                    else:
                        pe.wait_ge(pre_free, i * 2 + 1)
                    wide(i, s, 0, q_up, f, P, j, u_ps)
                    if s:
                        pe.wait_ge(lo_done, i * SALL + s)
                    wide(i, s, 1, q_gate, f, P, j, g_ps)

                def down0(j):
                    pe.wait_ge(lo_done, i * SALL + (j + 1) * FT0)
                    if j:
                        pe.wait_ge(down_free, i * 4 + 2)
                    for c in range(KC):
                        for f in range(FT0):
                            for w in range(2):
                                last = mm(acc[:, c, :], q_down[:, f, c * P:(c + 1) * P],
                                          hid0[:, (j * FT0 + f) % H_RING, w, :],
                                          start=(f == 0 and w == 0), stop=(f == FT0 - 1 and w == 1))
                        last.then_inc(down_ps, 1)

                def skip(c):
                    if c:
                        pe.wait_ge(y_free, i * 2 + c)
                    for j in range(NJ):
                        for q in range(NQ):
                            mm(y[q * CB:(q + 1) * CB, j, :], diag_d[:, c, q * CB:(q + 1) * CB],
                               xn[:, c, j * BLK:(j + 1) * BLK], start=True, stop=False, tile_position=(0, q * CB))

                def reduce(g):
                    pe.wait_ge(prod_done, i * UNITS + 4 * g + 4)
                    for j in range(NJ):
                        for q in range(NQ):
                            u = 4 * g + q
                            last = mm(y[q * CB:(q + 1) * CB, j, :], reduce_w[:, :],
                                      prod[:, u % PROD, j * BLK:(j + 1) * BLK], start=False, stop=(g % 4 == 3),
                                      tile_position=(0, q * CB))
                    last.then_inc(red_done, 1)

                if first:
                    pe.wait_ge(setup_dve, 2)
                for g in range(8):
                    if g == 0:
                        skip(0)
                    gated0(2 * g)
                    if g == 4:
                        down0(0)
                        skip(1)
                    gated0(2 * g + 1)
                    reduce(g)
                down0(1)

                pe.wait_ge(down_free, i * 4 + 4)
                for p in range(4):
                    if p >= 2:
                        pe.wait_ge(x2_tok, i * 4 + p - 1)
                    for t in range(2):
                        for c in range(KC):
                            tok = (2 * p + t) * P
                            last = nc.tensor.transpose(ug[:, p % 2, (t * KC + c) * P:(t * KC + c + 1) * P],
                                                       xt[:, c, tok:tok + P], ident[:, :])
                    last.then_inc(x2_ps, 1)
                to_channels(i, 1, x2tok)
                pe.wait_ge(xl_done, i * 8 + 8)
                if first:
                    pe.wait_ge(quant, 6)
                    pe.wait_ge(w_attn, 4 * 16)

                def gated1(s):
                    j, f = s // FT1, s % FT1
                    m = F1_LAST if f == FT1 - 1 else P
                    if s:
                        pe.wait_ge(th_done, i * SALL + S0 + s)
                    wide(i, S0 + s, 0, q_w1, f, m, j, u_ps)
                    if s:
                        pe.wait_ge(lo_done, i * SALL + S0 + s)
                    wide(i, S0 + s, 1, q_w2, f, m, j, g_ps)

                def q_proj(n):
                    c, j = n % 2, n // 2
                    if n >= 2:
                        pe.wait_ge(qe_done, i * 4 + n - 1)
                    for k in range(KC):
                        last = mm(xs[:, n % 2 * BLK:(n % 2 + 1) * BLK], wq_sb[:, k, c * P:(c + 1) * P],
                                  xn[:, k, j * BLK:(j + 1) * BLK], start=(k == 0), stop=(k == KC - 1))
                    last.then_inc(q_ps, 1)

                def kv_proj(t):
                    if t < 2:
                        pe.wait_ge(qe_done, i * 4 + 3 + t)
                    else:
                        pe.wait_ge(kv_sb, i * 8 + t - 1)
                    for k in range(KC):
                        last = mm(xs[:, t % 2 * BLK:(t % 2 + 1) * BLK], xn[:, k, t * P:(t + 1) * P],
                                  wkv_sb[:, k, :], start=(k == 0), stop=(k == KC - 1))
                    last.then_inc(kv_ps, 1)

                def kv_sum(t):
                    pe.wait_ge(kf_done, i * 8 + t + 1)
                    for c in range(KC):
                        last = mm(acc[:, c, 0:P + 1], kf[:, t % 2, c * P:(c + 1) * P], vx[:, t % 2, c, :],
                                  start=(t == 0), stop=(t == NT - 1))
                    last.then_inc(kv_acc, 1)

                for s in range(S1):
                    gated1(s)
                    if s < 4:
                        q_proj(s)
                    else:
                        kv_proj(s - 4)
                        if s >= 5:
                            kv_sum(s - 5)
                kv_sum(NT - 1)
                pe.wait_ge(kvx_done, i + 1)
                pe.wait_ge(qf_done, i * 4 + 4)

                def attend(t):
                    if t >= 2:
                        pe.wait_ge(otok_done, i * 8 + t - 1)
                    for c in range(KC):
                        last = mm(y[:, t % 2, c * OW:(c + 1) * OW], qf[:, c, t * P:(t + 1) * P], kvx[:, c, :],
                                  start=True, stop=True)
                    last.then_inc(o_ps, 1)

                def back(t):
                    pe.wait_ge(otok_done, i * 8 + t + 1)
                    if t == 4:
                        pe.wait_ge(ot_done, i * 2 + 1)
                    for c in range(KC):
                        last = nc.tensor.transpose(acc[:, c, t % 4 * P:(t % 4 + 1) * P],
                                                   otok[:, t % 2, c * P:(c + 1) * P], ident[:, :])
                    if t % 4 == 3:
                        last.then_inc(ot_ps, 1)

                for t in range(NT):
                    attend(t)
                    if t:
                        back(t - 1)
                back(NT - 1)
                pe.wait_ge(ot_done, i * 2 + 2)
                pe.wait_ge(lo_done, i * SALL + SALL)
                for j in range(NJ):
                    cut = slice(j * BLK, (j + 1) * BLK)
                    for c in range(KC):
                        if j:
                            pe.wait_ge(out_done, i * 4 + c + 1)
                        for k in range(KC):
                            mm(acc[:, c, :], wo_sb[:, k, c * P:(c + 1) * P], ot[:, k, cut],
                               start=(k == 0), stop=False)
                        for f in range(FT1):
                            m = F1_LAST if f == FT1 - 1 else P
                            for w in range(2):
                                last = mm(acc[:, c, :], q_w3[0:m, f, c * P:(c + 1) * P],
                                          hid1[0:m, j * FT1 + f, w, :], start=False,
                                          stop=(f == FT1 - 1 and w == 1))
                        last.then_inc(y2_ps, 1)

            batch(0, True)
            with pe.Fori(1, NBATCH) as i:
                batch(i, False)


def kernel(**inputs):
    import numpy as np
    import concourse.bacc as bacc
    from concourse.bass_utils import run_bass_kernel_spmd

    a = {k: np.asarray(v) for k, v in inputs.items()}
    put = np.ascontiguousarray
    x = a["L0_attn_input"]
    chan, row = np.arange(P), np.arange(P)
    arrays = {
        "x_tok": put(x),
        "x_cm": put(x.transpose(0, 2, 1)),
        "w_in": put(np.concatenate([a["L0_attn_W_dt_in"], a["L0_attn_W_B"], a["L0_attn_W_C"]]).T),
        "w_dt_out": put(a["L0_attn_W_dt_out"].T),
        "b_dt": put(a["L0_attn_b_dt_out"]),
        "d_skip": put(a["L0_attn_D"]),
        "a_log": put(a["L0_attn_A_log"].reshape(KC * NQ, CB, NSB, SB).transpose(1, 3, 0, 2).reshape(P, -1)),
        "w_up": put(a["L0_ffn_W_up"].T), "w_gate": put(a["L0_ffn_W_gate"].T), "w_down": put(a["L0_ffn_W_down"].T),
        "wq": put(a["L1_attn_wq"].T), "bq": put(a["L1_attn_bq"]),
        "wkv": put(np.concatenate([a["L1_attn_wk"], a["L1_attn_wv"]]).T),
        "bkv": put(np.concatenate([a["L1_attn_bk"], a["L1_attn_bv"]])),
        "wo": put(a["L1_attn_wo"].T), "bo": put(a["L1_attn_bo"]),
        "w1": put(a["L1_ffn_w1"].T), "w2": put(a["L1_ffn_w2"].T), "w3": put(a["L1_ffn_w3"].T),
        "ident": np.eye(P, dtype=np.float32),
        "reduce": put((chan[:, None] // SB == np.arange(CB)[None, :]).astype(np.float32)),
        "heads": put((chan[:, None] // DK == row[None, :] // DK).astype(np.float32)),
        "head_of": put((chan[:, None] // DK == np.arange(HPC)[None, :]).astype(np.float32)),
    }
    nc = bacc.Bacc("TRN2", target_bir_lowering=False, num_devices=1, dynamic_dma_scratch_size=1024)
    args = [nc.dram_tensor(f"in_{k}", v.shape, mybir.dt.from_np(v.dtype), kind="ExternalInput").ap()
            for k, v in arrays.items()]
    out = nc.dram_tensor("out_cm", (NBATCH, H, T), mybir.dt.float32, kind="ExternalOutput").ap()
    two_layer_kernel(nc, *args, out)
    r = run_bass_kernel_spmd(nc, [{f"in_{k}": v for k, v in arrays.items()}], core_ids=[0])
    return np.ascontiguousarray(r.results[0]["out_cm"].transpose(0, 2, 1))
```

```python
import concourse.bass as bass
from concourse import mybir
from contextlib import ExitStack

P = 128
NBATCH, T, H = 4, 1024, 256
BLK = 512
NJ = T // BLK
NT = T // P
KC = H // P
NS, RANK = 16, 64
CB, NQ, SB = 32, 4, 4
NSB = NS // SB
UNITS = KC * NSB * NQ
F0, F1 = 1024, 704
FT0, FT1 = F0 // P, -(-F1 // P)
F1_LAST = F1 - (FT1 - 1) * P
HEADS, DK = 16, 16
HPC = HEADS // KC
OW = P + HPC
LN_EPS, Q_EPS, DEN_EPS = 1e-5, 1e-8, 1e-8

X_SCALE = 2.0 ** 11
UP_Q = 2.0 ** -12
W2_Q = 2.0 ** -5
W3_Q = 2.0 ** -7

S0, S1 = NJ * FT0, NJ * FT1
GROUPS = NJ * KC * NSB
UPB = KC * NSB * NQ
UNITS = NJ * UPB
BT = BLK // P
HID0 = 11
RING = 3
PROD = 6
LEAD = 2
RAW1 = FT1 * H

FRONT = {1: 2, 0: 10}
TOKENS_G = (0, 2)
FFN1_G, KV_G, Q_G = 3, 3, 7
ATTEND_G = 9
DOWN_G = 9
OUT_GROUPS = {13: (0,), 14: (1,), 15: (2, 3)}
ADD_OUT = {14: (0,), 15: (1,)}


def at(batch, per_batch, n):
    i, back = batch
    return i * per_batch + (n - back * per_batch)


def slot0(s):
    return s if s < HID0 else s - FT0


def user_before(u, ring):
    if u >= ring:
        return u - ring
    return max(v for v in range(UNITS) if v % ring == u) - UNITS


def wait(engine, semaphore, count):
    if not isinstance(count, int) or count > 0:
        engine.wait_ge(semaphore, count)


def two_layer_kernel(nc, x_tok, x_cm, w_in, w_dt_out, b_dt, d_skip, a_log, w_up, w_gate, w_down,
                     wq, bq, wkv, bkv, wo, bo, w1, w2, w3, ident_in, reduce_in, heads_in, head_of_in, out):
    f32, f16 = mybir.dt.float32, mybir.dt.float16
    ALU, ACT = mybir.AluOpType, mybir.ActivationFunctionType

    with ExitStack() as ctx:
        def sb(name, shape, dt=f32):
            return ctx.enter_context(nc.sbuf_tensor(name, shape, dt))

        def ps(name, shape):
            return ctx.enter_context(nc.psum_tensor(name, shape, f32))

        def sem(name):
            return ctx.enter_context(nc.semaphore(name))

        q_up = sb("q_up", [P, KC, F0], f16)
        q_gate = sb("q_gate", [P, KC, F0], f16)
        q_down = sb("q_down", [P, FT0, H], f16)
        q_w1 = sb("q_w1", [P, KC, F1], f16)
        q_w2 = sb("q_w2", [P, KC, F1], f16)
        q_w3 = sb("q_w3", [P, FT1, H], f16)
        win_sb = sb("win_sb", [P, KC, RANK + 2 * NS])
        wdt_sb = sb("wdt_sb", [RANK, H])
        wq_sb = sb("wq_sb", [P, KC, H])
        wkv_sb = sb("wkv_sb", [P, KC, 2 * H])
        wo_sb = sb("wo_sb", [P, KC, H])
        bkv_sb = sb("bkv_sb", [P, 2 * H])
        cols = sb("cols", [P, 4, KC])
        a_neg = sb("a_neg", [P, KC * NQ * NSB])
        ident = sb("ident", [P, P])
        reduce_w = sb("reduce_w", [P, CB])
        diag_d = sb("diag_d", [P, KC, P])
        heads = sb("heads", [P, P])
        head_of = sb("head_of", [P, HPC])
        neg_half = sb("neg_half", [P, NT])
        eps = sb("eps", [P, NT])
        spare = sb("spare", [P, 2])
        scale_sb = sb("scale_sb", [P, 5, 6])
        sdown = sb("sdown", [P, 2])

        xtok = sb("xtok", [P, BT, H])
        xt = sb("xt", [P, NJ, KC, BLK])
        xn0 = sb("xn0", [P, NJ, KC, BLK])
        xh0 = sb("xh0", [P, NJ, KC, BLK], f16)
        xl0 = sb("xl0", [P, NJ, KC, BLK], f16)
        lbc = sb("lbc", [RANK + 2 * NS, BLK])
        dt_sb = sb("dt_sb", [P, KC, BLK])
        dtu = sb("dtu", [P, KC, BLK])
        bc = sb("bc", [P, 2, NSB, BLK])
        dtb = sb("dtb", [P, 2, NQ, BLK])
        a_ring = sb("a_ring", [P, RING, BLK])
        b_ring = sb("b_ring", [P, RING, BLK])
        prod = sb("prod", [P, PROD, BLK])
        carry = sb("carry", [P, UPB])
        th0 = sb("th0", [P, 2, BLK])
        hid0 = sb("hid0", [P, HID0, 2, BLK], f16)
        x2 = sb("x2", [P, KC, T])
        wide1 = sb("wide1", [P, 3 * KC * T])
        xn1 = wide1[:, 0:KC * T].rearrange("p (c t) -> p c t", c=KC)
        qf = wide1[:, KC * T:2 * KC * T].rearrange("p (c t) -> p c t", c=KC)
        parts1 = wide1[:, 2 * KC * T:3 * KC * T].bitcast(f16).rearrange("p (w c t) -> p w c t", w=2, c=KC)
        xh1, xl1 = parts1[:, 0], parts1[:, 1]
        hid1_raw = sb("hid1_raw", [P, S1 * BLK])
        hid1 = hid1_raw[:, :].bitcast(f16).rearrange("p (s w t) -> p s w t", s=S1, w=2)
        x2tok = hid1_raw[:, 0:NT * H].rearrange("p (t h) -> p t h", h=H)
        th1 = sb("th1", [P, 2, BLK])
        ones = th1[:, 0, 0:P]
        q_min = sb("q_min", [P, 2, BLK])
        k_all = qf[:, 0, :].rearrange("p (w r t) -> p w r t", w=2, r=2)
        kf = q_min[:, 0, :].rearrange("p (r t) -> p r t", r=2)
        otok = q_min[:, 1, :].rearrange("p (r t) -> p r t", r=2)
        den = sb("den", [P, 2, 2, HEADS])
        ksum = sb("ksum", [P, KC])
        vx = sb("vx", [P, 2, KC, P + 1])
        kvx = sb("kvx", [P, KC, OW])
        stats = sb("stats", [P, NT, 6])
        mv = [sb(f"mv{l}", [P, NT, 2]) for l in range(2)]
        rstd = [sb(f"rstd{l}", [P, 2, NT]) for l in range(2)]
        raw0 = hid1_raw[:, 0:3 * KC * F0].rearrange("p (w n) -> p w n", w=3)
        raw1 = wide1[:, 0:3 * RAW1].rearrange("p (w n) -> p w n", w=3)
        hid0_flat = hid0[:, :, :, :].rearrange("p s w t -> p (s w t)")
        cmp_lo, cmp_hi = hid0_flat[:, 0:KC * F0], hid0_flat[:, KC * F0:2 * KC * F0]
        junk = x2[:, :, :].rearrange("p c t -> p (c t)")

        pa = ps("pa", [P, 2, BLK])
        pb = ps("pb", [P, 2, BLK])
        acc = ps("acc", [P, 2, BLK])
        xs = ps("xs", [P, BLK])
        y = ps("y", [P, BLK])

        w_small = sem("w_small"); w_raw0 = sem("w_raw0"); w_raw1 = sem("w_raw1"); w_attn = sem("w_attn")
        raw_tail = sem("raw_tail"); const_set = sem("const_set"); abs_done = sem("abs_done")
        sums_ps = sem("sums_ps"); setup_dve = sem("setup_dve"); setup_self = sem("setup_self")
        quant = sem("quant"); aneg_done = sem("aneg_done")
        xtok_in = sem("xtok_in")
        xt_in = [sem(f"xt_in{j}") for j in range(NJ)]
        stats0 = sem("stats0"); agg0 = sem("agg0"); rstd0 = sem("rstd0")
        xn_tok0 = sem("xn_tok0")
        xnt_ps0 = sem("xnt_ps0")
        xh_done0 = sem("xh_done0")
        xl_done0 = sem("xl_done0")
        low_ps = sem("low_ps"); low_sb = sem("low_sb")
        pre_ps = sem("pre_ps"); pre_free = sem("pre_free")
        sp_abs = sem("sp_abs"); sp_exp = sem("sp_exp"); sp_parts = sem("sp_parts")
        dt_sum = sem("dt_sum"); dt_done = sem("dt_done")
        bc_dram = sem("bc_dram")
        bc_in = [sem(f"bc_in{n}") for n in range(NSB)]
        dtb_in = [sem(f"dtb_in{n}") for n in range(NQ)]
        a_done = sem("a_done"); b_done = sem("b_done"); scan_done = sem("scan_done"); prod_done = sem("prod_done")
        red_done = sem("red_done")
        y_free = sem("y_free")
        u0_ps = sem("u0_ps"); g0_ps = sem("g0_ps"); th0_done = sem("th0_done"); t1_done = sem("t1_done")
        r0_done = sem("r0_done"); hi0_done = sem("hi0_done"); lo0_done = sem("lo0_done")
        down_ps = sem("down_ps"); x2_done = sem("x2_done")
        x2_ps = sem("x2_ps"); x2_tok = sem("x2_tok")
        stats1 = sem("stats1"); agg1 = sem("agg1"); rstd1 = sem("rstd1")
        xn_tok1 = sem("xn_tok1")
        xnt_ps1 = sem("xnt_ps1"); xh_done1 = sem("xh_done1"); xl_done1 = sem("xl_done1")
        q_ps = sem("q_ps"); qm_done = sem("qm_done"); qe_done = sem("qe_done"); qf_done = sem("qf_done")
        kv_ps = sem("kv_ps"); kv_sb = sem("kv_sb"); km_done = sem("km_done"); ke_done = sem("ke_done")
        kf_done = sem("kf_done"); kv_acc = sem("kv_acc")
        ksum_done = sem("ksum_done"); kvx_done = sem("kvx_done")
        u1_ps = sem("u1_ps"); g1_ps = sem("g1_ps"); th1_done = sem("th1_done")
        r1_done = sem("r1_done"); hi1_done = sem("hi1_done"); lo1_done = sem("lo1_done")
        o_ps = sem("o_ps"); den_done = sem("den_done"); otok_done = sem("otok_done")
        ot_ps = sem("ot_ps"); ot_done = sem("ot_done")
        y2_ps = sem("y2_ps"); out_done = sem("out_done")
        out_dram = [sem(f"out_dram{j}") for j in range(NJ)]
        rstd_self = sem("rstd_self")

        scratch = nc.dram_tensor("bc_scratch", (2 * NS, BLK), f32, kind="Internal").ap()
        block = ctx.enter_context(nc.Block())

        def step_of_unit(u):
            return u // UPB, u % UPB // (NSB * NQ), u // NQ % NSB, u % NQ

        def rows1(s):
            return F1_LAST if s % FT1 == FT1 - 1 else P

        @block.sync
        def _(sp):
            sp.dma_start(xtok[:, :, :], x_tok[0, 0:BLK].rearrange("(t p) h -> p t h", p=P)).then_inc(xtok_in, 16)
            for dst, src in ((ident[:, :], ident_in), (reduce_w[:, :], reduce_in), (heads[:, :], heads_in),
                             (head_of[:, :], head_of_in), (a_neg[:, :], a_log),
                             (win_sb[:, :, :], w_in.rearrange("(k p) m -> p k m", p=P)), (wdt_sb[:, :], w_dt_out),
                             (cols[:, 0, :], b_dt.rearrange("(k p) -> p k", p=P)),
                             (cols[:, 1, :], d_skip.rearrange("(k p) -> p k", p=P)),
                             (cols[:, 2, :], bq.rearrange("(k p) -> p k", p=P)),
                             (cols[:, 3, :], bo.rearrange("(k p) -> p k", p=P))):
                with nc.allow_non_contiguous_dma(reason="a few short columns"):
                    sp.dma_start(dst, src).then_inc(w_small, 16)
            for n, w in enumerate((w_up, w_gate, w_down)):
                sp.dma_start(raw0[:, n, :].rearrange("p (k m) -> p k m", k=w.shape[0] // P),
                             w.rearrange("(k p) m -> p k m", p=P)).then_inc(w_raw0, 16)
            for n, w in enumerate((w1, w2)):
                sp.dma_start(raw1[:, n, 0:KC * F1].rearrange("p (k m) -> p k m", k=KC),
                             w.rearrange("(k p) m -> p k m", p=P)).then_inc(w_raw1, 16)
            full = (FT1 - 1) * P
            sp.dma_start(raw1[:, 2, 0:(FT1 - 1) * H].rearrange("p (k m) -> p k m", k=FT1 - 1),
                         w3[0:full, :].rearrange("(k p) m -> p k m", p=P)).then_inc(w_raw1, 16)
            sp.dma_start(raw1[0:F1_LAST, 2, (FT1 - 1) * H:FT1 * H], w3[full:F1, :]).then_inc(w_raw1, 16)
            for dst, src in ((wq_sb, wq), (wkv_sb, wkv), (wo_sb, wo)):
                sp.dma_start(dst[:, :, :], src.rearrange("(k p) m -> p k m", p=P)).then_inc(w_attn, 16)
            sp.dma_start(bkv_sb[:, :], bkv.rearrange("(a n) -> a n", a=1).to_broadcast([P, 2 * H])).then_inc(w_attn, 16)

            def layer0(i, first, last):
                b = (i, 0)

                def count(per_batch, n):
                    return n if first else sp.to_reg(at(b, per_batch, n))

                def tokens(batch, j, transposed):
                    sp.wait_ge(xnt_ps0, transposed)
                    sp.dma_start(xtok[:, :, :],
                                 x_tok[batch, j * BLK:(j + 1) * BLK].rearrange("(t p) h -> p t h", p=P))\
                      .then_inc(xtok_in, 16)

                def stream(j):
                    sp.dma_start(xt[:, j, :, :],
                                 x_cm[i, :, j * BLK:(j + 1) * BLK].rearrange("(k p) t -> p k t", p=P))\
                      .then_inc(xt_in[j], 16)

                def states(j, nb):
                    if j or not first:
                        sp.wait_ge(b_done, bc_used[j][nb])
                        sp.wait_ge(prod_done, bc_used[j][nb])
                    if nb == 0:
                        sp.wait_ge(bc_dram, in_dram[j])
                    for w in range(2):
                        row = w * NS + nb * SB
                        sp.dma_start(bc[:, w, nb, :],
                                     scratch[row:row + SB, :].unsqueeze(0).to_broadcast([CB, SB, BLK]))\
                          .then_inc(bc_in[nb], 16)

                transposed, moved = [count(4, 2), count(4, 4)], [count(4, 2 * j - 2) for j in range(NJ)]
                low_ready, in_dram = [count(2, j + 1) for j in range(NJ)], [count(32, 16 * j + 16) for j in range(NJ)]
                steps = [count(4, k + 1) for k in range(NJ * KC)]
                scratch_read = [count(64, 32 * j) for j in range(NJ)]
                bc_used = [[count(UNITS, (j - 1) * UPB + (NSB + nb + 1) * NQ) for nb in range(NSB)] for j in range(NJ)]
                dtb_used = [[count(UNITS, k * 16 - NQ + q + 1) for q in range(NQ)] for k in range(NJ * KC)]
                for j in range(NJ):
                    if j or not first:
                        for nb in range(NSB):
                            sp.wait_ge(bc_in[nb], scratch_read[j])
                    if j == 0:
                        tokens(i, 1, transposed[0])
                    sp.wait_ge(low_sb, low_ready[j])
                    sp.dma_start(scratch, lbc[RANK:RANK + 2 * NS, :]).then_inc(bc_dram, 16)
                    if j == 1 and not last:
                        tokens(i + 1, 0, transposed[1])
                    for nb in range(NSB - 1):
                        states(j, nb)
                    for c in range(KC):
                        k = j * KC + c
                        sp.wait_ge(dt_done, steps[k])
                        for q in range(NQ):
                            if k or not first:
                                sp.wait_ge(a_done, dtb_used[k][q])
                                sp.wait_ge(b_done, dtb_used[k][q])
                            for w, src in enumerate((dt_sb, dtu)):
                                if q == NQ - 1 and w == 1 and k < NJ and not first:
                                    sp.wait_ge(x2_done, moved[k])
                                sp.dma_start(dtb[:, w, q, :],
                                             src[q * CB:(q + 1) * CB, c, :].unsqueeze(1).to_broadcast([CB, SB, BLK]))\
                                  .then_inc(dtb_in[q], 16)
                        if c == 0:
                            states(j, NSB - 1)
                        if k < NJ:
                            stream(k)

            layer0(0, True, False)
            with sp.Fori(1, NBATCH - 1) as i:
                layer0(i, False, False)
            layer0(NBATCH - 1, False, True)
            for j in range(NJ):
                sp.wait_ge(out_dram[j], NBATCH * 32)
            sp.wait_ge(bc_dram, NBATCH * 32)

        @block.scalar
        def _(act):
            act.wait_ge(w_small, 11 * 16)
            nc.scalar.activation(a_neg[:, :], a_neg[:, :], ACT.Exp).then_inc(aneg_done, 1)

            def magnitudes(layer):
                if layer == 0:
                    act.wait_ge(w_raw0, 3 * 16)
                else:
                    act.wait_ge(w_raw1, 4 * 16)
                    act.wait_ge(raw_tail, 1)
                for n in range(3):
                    raw = (raw0, raw1)[layer]
                    m = (KC * F0, KC * F0, FT0 * H, KC * F1, KC * F1, RAW1)[3 * layer + n]
                    nc.scalar.activation(junk[:, 0:m], raw[:, n, 0:m], ACT.Abs,
                                         accum_out=scale_sb[:, 0, 3 * layer + n:3 * layer + n + 1])\
                        .then_inc(abs_done, 1)
                    act.wait_ge(abs_done, 3 * layer + n + 1)

            def front_steps(b, first=False):
                def parts0(j):
                    for c in range(KC):
                        act.wait_ge(xnt_ps0, at(b, 4, 2 * j + c + 1))
                        nc.scalar.activation(xn0[:, j, c, :], pa[:, c, :], ACT.Copy)
                        nc.scalar.activation(xh0[:, j, c, :], pa[:, c, :], ACT.Copy, scale=X_SCALE).then_inc(xh_done0, 1)

                def low(j):
                    act.wait_ge(low_ps, at(b, 2, j + 1))
                    nc.scalar.activation(lbc[:, :], pa[0:RANK + 2 * NS, 0, :], ACT.Copy).then_inc(low_sb, 1)

                def softplus_parts(j):
                    for c in range(KC):
                        k = 2 * j + c
                        act.wait_ge(pre_ps, at(b, 4, k + 1))
                        if k or not first:
                            for q in range(NQ):
                                wait(act, dtb_in[q], at(b, 128, 64 * j))
                        nc.scalar.activation(dt_sb[:, c, :], pa[:, c, :], ACT.Abs, bias=cols[:, 0, c:c + 1])\
                            .then_inc(sp_abs, 1)
                        nc.scalar.activation(dtu[:, c, :], pa[:, c, :], ACT.Relu, bias=cols[:, 0, c:c + 1])\
                            .then_inc(pre_free, 1)

                def softplus_exp(j):
                    for c in range(KC):
                        act.wait_ge(sp_abs, at(b, 4, 2 * j + c + 1))
                        nc.scalar.activation(dt_sb[:, c, :], dt_sb[:, c, :], ACT.Exp, scale=-1.0).then_inc(sp_exp, 1)

                def softplus_ln(j):
                    for c in range(KC):
                        act.wait_ge(sp_exp, at(b, 4, 2 * j + c + 1))
                        nc.scalar.activation(dt_sb[:, c, :], dt_sb[:, c, :], ACT.Ln, bias=1.0).then_inc(sp_parts, 1)

                return parts0, low, softplus_parts, softplus_exp, softplus_ln

            def decay(b, u, first=False):
                j, c, nb, q = step_of_unit(u)
                act.wait_ge(dtb_in[q], at(b, 128, (j * KC + c + 1) * 32))
                if u >= RING or not first:
                    wait(act, scan_done, at(b, UNITS, user_before(u, RING) + 1))
                k = (c * NQ + q) * NSB + nb
                nc.scalar.activation(a_ring[:, u % RING, :], dtb[:, 0, q, :], ACT.Exp,
                                     scale=a_neg[:, k:k + 1]).then_inc(a_done, 1)

            def body(i, l0, l1, more, first=False):
                b, m = (i, 0), (i, 1)
                fronts = {1: front_steps(b), 0: front_steps((i, -1))}

                def decay_ahead(u):
                    if u + LEAD < UNITS:
                        decay(b, u + LEAD, first)
                    elif more:
                        decay((i, -1), u + LEAD - UNITS)

                def tanh0(s):
                    act.wait_ge(u0_ps, at(b, S0, s + 1))
                    if s >= 2 or not first:
                        wait(act, lo0_done, at(b, S0, s - 1))
                    nc.scalar.activation(th0[:, s % 2, :], pa[:, 0, :], ACT.Tanh, scale=scale_sb[:, 2, 0:1])\
                        .then_inc(th0_done, 1)

                def high0(s):
                    act.wait_ge(r0_done, at(b, S0, s + 1))
                    if s >= HID0 or not first:
                        act.wait_ge(down_ps, at(b, 4, 2 if s >= HID0 else 0 if s >= HID0 - FT0 else -2))
                    nc.scalar.activation(hid0[:, slot0(s), 0, :], th0[:, s % 2, :], ACT.Copy).then_inc(hi0_done, 1)

                def tokens1(p):
                    act.wait_ge(x2_ps, at(m, 4, p + 1))
                    nc.scalar.activation(x2tok[:, 2 * p:2 * p + 2, :],
                                         pb[:, p % 2, :].rearrange("p (t h) -> p t h", t=2), ACT.Copy)\
                        .then_inc(x2_tok, 1)

                def parts1_of(j):
                    for c in range(KC):
                        cut = slice(j * BLK, (j + 1) * BLK)
                        act.wait_ge(xnt_ps1, at(m, 4, 2 * j + c + 1))
                        nc.scalar.activation(xn1[:, c, cut], pb[:, c, :], ACT.Copy)
                        nc.scalar.activation(xh1[:, c, cut], pb[:, c, :], ACT.Copy, scale=X_SCALE)\
                            .then_inc(xh_done1, 1)

                def q_feature(n):
                    c, j = n % 2, n // 2
                    act.wait_ge(qm_done, at(m, 4, n + 1))
                    nc.scalar.activation(qf[:, c, j * BLK:(j + 1) * BLK], pb[:, n % 2, :], ACT.Relu,
                                         bias=cols[:, 2, c:c + 1])
                    nc.scalar.activation(q_min[:, n % 2, :], q_min[:, n % 2, :], ACT.Exp).then_inc(qe_done, 1)

                def k_feature(t):
                    act.wait_ge(km_done, at(m, 8, t + 1))
                    nc.scalar.activation(k_all[:, 1, t % 2, :], k_all[:, 1, t % 2, :], ACT.Exp).then_inc(ke_done, 1)

                def tanh1(s):
                    act.wait_ge(u1_ps, at(m, S1, s + 1))
                    if s >= 2:
                        act.wait_ge(lo1_done, at(m, S1, s - 1))
                    nc.scalar.activation(th1[0:rows1(s), s % 2, :], pb[0:rows1(s), 0, :], ACT.Tanh).then_inc(th1_done, 1)

                def high1(s):
                    act.wait_ge(r1_done, at(m, S1, s + 1))
                    nc.scalar.activation(hid1[0:rows1(s), s, 0, :], th1[0:rows1(s), s % 2, :], ACT.Copy)\
                        .then_inc(hi1_done, 1)

                def attended(p):
                    act.wait_ge(ot_ps, at(m, 4, p + 1))
                    nc.scalar.activation(qf[:, :, 2 * p * P:(2 * p + 2) * P],
                                         pb[:, 0, :].rearrange("p (c t) -> p c t", c=KC), ACT.Copy)\
                        .then_inc(ot_done, 1)

                def store(n):
                    j, c = n // KC, n % KC
                    act.wait_ge(out_done, at(m, 4, n + 1))
                    act.dma_start(out[m[0] - m[1], c * P:(c + 1) * P, j * BLK:(j + 1) * BLK],
                                  xn1[:, c, j * BLK:(j + 1) * BLK]).then_inc(out_dram[j], 16)

                for g in range(GROUPS):
                    s1 = g - FFN1_G if l1 and 0 <= g - FFN1_G < S1 else None
                    if l0:
                        decay_ahead(4 * g)
                        for j, f in FRONT.items():
                            if (j or more) and g == f + 4:
                                fronts[j][2](j)
                        tanh0(g)
                    if l1:
                        if g == TOKENS_G[0]:
                            tokens1(0)
                            tokens1(1)
                        for j in range(NJ):
                            if g == TOKENS_G[j] + 2:
                                parts1_of(j)
                        for t in range(2 * (g - KV_G - 1), 2 * (g - KV_G)):
                            if 0 <= t < NT:
                                k_feature(t)
                        for n in range(2 * (g - Q_G - 1), 2 * (g - Q_G)):
                            if 0 <= n < 4:
                                q_feature(n)
                    if l0:
                        decay_ahead(4 * g + 1)
                    if s1 is not None:
                        tanh1(s1)
                    if l0:
                        high0(g)
                        decay_ahead(4 * g + 2)
                    if s1 is not None:
                        high1(s1)
                    if l1 and 0 <= g - ATTEND_G - 1 < NT // 2:
                        attended(g - ATTEND_G - 1)
                    if l0:
                        for j, f in FRONT.items():
                            if (j or more) and g == f + 4:
                                fronts[j][3](j)
                        decay_ahead(4 * g + 3)
                        for j, f in FRONT.items():
                            if (j or more) and g == f + 1:
                                fronts[j][0](j)
                            if (j or more) and g == f + 2:
                                fronts[j][1](j)
                            if (j or more) and g == f + 4:
                                fronts[j][4](j)
                    if l1:
                        if g == TOKENS_G[1]:
                            tokens1(2)
                            tokens1(3)
                        for n in ADD_OUT.get(g, ()):
                            store(n)
                if l1:
                    store(2)
                    store(3)
                    for j in range(NJ):
                        act.wait_ge(out_dram[j], at(m, 32, 32))

            parts0, low, softplus_parts, softplus_exp, softplus_ln = front_steps((0, 0), first=True)
            parts0(0)
            low(0)
            magnitudes(0)
            softplus_parts(0)
            softplus_exp(0)
            softplus_ln(0)
            magnitudes(1)
            act.wait_ge(setup_dve, 2)
            for u in range(LEAD):
                decay((0, 0), u, first=True)
            body(0, True, False, True, first=True)
            with act.Fori(1, NBATCH - 1) as i:
                body(i, True, True, True)
            body(NBATCH - 1, True, True, False)
            body(NBATCH, False, True, False)

        @block.gpsimd
        def _(pool):
            nc.gpsimd.memset(raw1[F1_LAST:P, 2, (FT1 - 1) * H:FT1 * H], 0.0).then_inc(raw_tail, 1)
            pool.wait_ge(raw_tail, 1)
            nc.gpsimd.memset(neg_half[:, :], -0.5)
            nc.gpsimd.memset(eps[:, :], LN_EPS)
            nc.gpsimd.memset(vx[:, :, :, P:P + 1], 1.0)
            nc.gpsimd.memset(ones, 1.0).then_inc(const_set, 1)
            pool.wait_ge(const_set, 1)

            def front_steps(b, self_n):
                def power(l, tiles, ready, ready_n, done, self_n):
                    pool.wait_ge(ready, ready_n)
                    nc.gpsimd.tensor_tensor(out=rstd[l][:, 0, tiles], in0=mv[l][:, tiles, 1], in1=eps[:, tiles],
                                            op=ALU.add).then_inc(rstd_self, 1)
                    pool.wait_ge(rstd_self, self_n)
                    nc.gpsimd.tensor_tensor(out=rstd[l][:, 1, tiles], in0=rstd[l][:, 0, tiles],
                                            in1=neg_half[:, tiles], op=ALU.pow).then_inc(done, 1)

                def rstd_of0(j):
                    power(0, slice(j * BT, (j + 1) * BT), agg0, at(b, 2, j + 1), rstd0, self_n)

                def time_step(j):
                    for c in range(KC):
                        k = 2 * j + c
                        pool.wait_ge(sp_parts, at(b, 4, k + 1))
                        nc.gpsimd.tensor_tensor(out=dt_sb[:, c, :], in0=dt_sb[:, c, :], in1=dtu[:, c, :], op=ALU.add)\
                            .then_inc(dt_sum, 1)
                        pool.wait_ge(dt_sum, at(b, 4, k + 1))
                        nc.gpsimd.tensor_tensor(out=dtu[:, c, :], in0=dt_sb[:, c, :], in1=xn0[:, j, c, :], op=ALU.mult)\
                            .then_inc(dt_done, 1)

                return power, rstd_of0, time_step

            def into_state(b, u, first=False):
                j, c, nb, q = step_of_unit(u)
                pool.wait_ge(dtb_in[q], at(b, 128, (j * KC + c + 1) * 32))
                pool.wait_ge(bc_in[nb], at(b, 64, 32 * j + 32))
                if u >= RING or not first:
                    wait(pool, scan_done, at(b, UNITS, user_before(u, RING) + 1))
                nc.gpsimd.tensor_tensor(out=b_ring[:, u % RING, :], in0=dtb[:, 1, q, :], in1=bc[:, 0, nb, :],
                                        op=ALU.mult).then_inc(b_done, 1)

            def body(i, l0, l1, more, first=False):
                b, m = (i, 0), (i, 1)
                power, _, _ = front_steps(m, None)
                fronts = {1: front_steps(b, 2 if first else at(b, 4, 1)),
                          0: front_steps((i, -1), 3 if first else at(b, 4, 3))}

                def rstd_of1(j):
                    power(1, slice(j * BT, (j + 1) * BT), agg1, at(m, 2, j + 1), rstd1,
                          at(b, 4, 2 * j if l0 else j - 1))

                def into_state_ahead(u):
                    if u + LEAD < UNITS:
                        into_state(b, u + LEAD, first)
                    elif more:
                        into_state((i, -1), u + LEAD - UNITS)

                def q_sum(n):
                    c, j = n % 2, n // 2
                    pool.wait_ge(qe_done, at(m, 4, n + 1))
                    part = qf[:, c, j * BLK:(j + 1) * BLK]
                    nc.gpsimd.tensor_tensor(out=part, in0=part, in1=q_min[:, n % 2, :], op=ALU.add)\
                        .then_inc(qf_done, 1)

                def low0(b, s):
                    pool.wait_ge(hi0_done, at(b, S0, s + 1))
                    nc.gpsimd.tensor_tensor(out=hid0[:, slot0(s), 1, :], in0=th0[:, s % 2, :],
                                            in1=hid0[:, slot0(s), 0, :], op=ALU.subtract).then_inc(lo0_done, 1)

                def low1(s):
                    rows = rows1(s)
                    pool.wait_ge(hi1_done, at(m, S1, s + 1))
                    nc.gpsimd.tensor_tensor(out=hid1[0:rows, s, 1, :], in0=th1[0:rows, s % 2, :],
                                            in1=hid1[0:rows, s, 0, :], op=ALU.subtract).then_inc(lo1_done, 1)

                for g in range(GROUPS):
                    if l0:
                        into_state_ahead(4 * g)
                    if g == 0 and l1:
                        low0(m, S0 - 1)
                    if l1:
                        for j in range(NJ):
                            if g == TOKENS_G[j] + 1:
                                rstd_of1(j)
                    if l0:
                        into_state_ahead(4 * g + 1)
                        if g:
                            low0(b, g - 1)
                        into_state_ahead(4 * g + 2)
                    if l1 and 0 <= g - 1 - FFN1_G < S1:
                        low1(g - 1 - FFN1_G)
                    if l1:
                        for n in range(2 * (g - Q_G - 1), 2 * (g - Q_G)):
                            if 0 <= n < 4:
                                q_sum(n)
                    if l0:
                        into_state_ahead(4 * g + 3)
                        for j, f in FRONT.items():
                            _, rstd_of0, time_step = fronts[j]
                            if (j or more) and g == f:
                                rstd_of0(j)
                            if (j or more) and g == f + 4:
                                time_step(j)

            _, rstd_of0, time_step = front_steps((0, 0), 1)
            rstd_of0(0)
            time_step(0)
            for u in range(LEAD):
                into_state((0, 0), u, first=True)
            body(0, True, False, True, first=True)
            with pool.Fori(1, NBATCH - 1) as i:
                body(i, True, True, True)
            body(NBATCH - 1, True, True, False)
            body(NBATCH, False, True, False)

        @block.vector
        def _(dve):
            def moments(l, tok, tiles, stat_sem, stat_n, agg_sem):
                for t in tiles:
                    last = nc.vector.bn_stats(stats[:, t, :], tok[:, t % tok.shape[1], :])
                last.then_inc(stat_sem, 1)
                dve.wait_ge(stat_sem, stat_n)
                nc.vector.memset(spare[:, :], 0.0)
                for t in tiles:
                    last = nc.vector.bn_aggr(mv[l][:, t, :], stats[:, t, :])
                last.then_inc(agg_sem, 1)

            def normalise(l, tok, tiles, done):
                for t in tiles:
                    tile = tok[:, t % tok.shape[1], :]
                    nc.vector.tensor_scalar(tile, tile, mv[l][:, t, 0:1], rstd[l][:, 1, t:t + 1],
                                            ALU.subtract, ALU.mult).then_inc(done, 1)

            def setup():
                dve.wait_ge(w_small, 11 * 16)
                for c in range(KC):
                    nc.vector.tensor_scalar(diag_d[:, c, :], ident[:, :], cols[:, 1, c:c + 1], None, ALU.mult)
                dve.wait_ge(aneg_done, 1)
                nc.vector.tensor_scalar(a_neg[:, :], a_neg[:, :], -1.0, None, ALU.mult).then_inc(setup_dve, 1)

            chain = [0]

            def link(ins):
                chain[0] += 1
                ins.then_inc(setup_self, 1)
                dve.wait_ge(setup_self, chain[0])

            def thresholds():
                dve.wait_ge(sums_ps, 1)
                link(nc.vector.tensor_scalar(scale_sb[:, 1, 0:3], y[:, 0:3], 1.0 / (F0 * H), None, ALU.mult))
                link(nc.vector.tensor_scalar(scale_sb[:, 1, 3:6], y[:, 3:6], 1.0 / (F1 * H), None, ALU.mult))
                link(nc.vector.tensor_scalar(scale_sb[:, 2, :], scale_sb[:, 1, :], Q_EPS, None, ALU.add))
                nc.vector.tensor_scalar(scale_sb[:, 3, :], scale_sb[:, 2, :], 0.5, None, ALU.mult)
                link(nc.vector.tensor_scalar(scale_sb[:, 4, :], scale_sb[:, 2, :], -0.5, None, ALU.mult))
                link(nc.vector.tensor_tensor(out=sdown[:, 0:1], in0=scale_sb[:, 2, 0:1], in1=scale_sb[:, 2, 1:2],
                                             op=ALU.mult))
                nc.vector.scalar_tensor_tensor(out=sdown[:, 1:2], in0=sdown[:, 0:1], scalar=2.0,
                                               in1=scale_sb[:, 2, 2:3], op0=ALU.mult, op1=ALU.mult)\
                    .then_inc(setup_dve, 1)

            def quantise(n, dst, src, size, q):
                nc.vector.tensor_scalar(cmp_lo[:, 0:size], src, scale_sb[:, 4, n:n + 1], q, ALU.is_lt, ALU.mult)
                link(nc.vector.tensor_scalar(cmp_hi[:, 0:size], src, scale_sb[:, 3, n:n + 1], q, ALU.is_gt, ALU.mult))
                nc.vector.tensor_tensor(out=dst, in0=cmp_hi[:, 0:size], in1=cmp_lo[:, 0:size], op=ALU.subtract)\
                    .then_inc(quant, 1)
                dve.wait_ge(quant, n + 1)

            def flat(w):
                return w[:, :, :].rearrange("p k m -> p (k m)")

            def front_steps(b):
                def moments0(j):
                    dve.wait_ge(xtok_in, at(b, 32, 16 * j + 16))
                    moments(0, xtok, range(j * BT, (j + 1) * BT), stats0, at(b, 2, j + 1), agg0)

                def normalise0(j):
                    dve.wait_ge(rstd0, at(b, 2, j + 1))
                    normalise(0, xtok, range(j * BT, (j + 1) * BT), xn_tok0)

                def low_part0(j):
                    for c in range(KC):
                        dve.wait_ge(xh_done0, at(b, 4, 2 * j + c + 1))
                        nc.vector.scalar_tensor_tensor(out=xl0[:, j, c, :], in0=pa[:, c, :], scalar=X_SCALE,
                                                       in1=xh0[:, j, c, :], op0=ALU.mult, op1=ALU.subtract)\
                            .then_inc(xl_done0, 1)

                return moments0, normalise0, low_part0

            def body(i, l0, l1, more, first=False):
                b, m = (i, 0), (i, 1)
                fronts = {1: front_steps(b), 0: front_steps((i, -1))}

                def unit(u):
                    j, c, nb, q = step_of_unit(u)
                    v = u % UPB
                    dve.wait_ge(a_done, at(b, UNITS, u + 1))
                    dve.wait_ge(b_done, at(b, UNITS, u + 1))
                    wait(dve, prod_done, at(b, UNITS, u))
                    nc.vector.tensor_tensor_scan(out=xs[:, :], data0=a_ring[:, u % RING, :],
                                                 data1=b_ring[:, u % RING, :],
                                                 initial=carry[:, v:v + 1] if j else 0.0,
                                                 op0=ALU.mult, op1=ALU.add).then_inc(scan_done, 1)
                    if u >= PROD or not first:
                        wait(dve, red_done, at(b, GROUPS, user_before(u, PROD) // 4 + 1))
                    dve.wait_ge(bc_in[nb], at(b, 64, 32 * j + 32))
                    dve.wait_ge(scan_done, at(b, UNITS, u + 1))
                    if j == 0:
                        nc.vector.tensor_copy(carry[:, v:v + 1], xs[:, BLK - 1:BLK])
                    nc.vector.tensor_tensor(out=prod[:, u % PROD, :], in0=xs[:, :], in1=bc[:, 1, nb, :],
                                            op=ALU.mult).then_inc(prod_done, 1)

                def gate0(s):
                    slot = th0[:, s % 2, :]
                    dve.wait_ge(th0_done, at(b, S0, s + 1))
                    nc.vector.scalar_tensor_tensor(out=slot, in0=slot, scalar=1.0, in1=pa[:, 0, :],
                                                   op0=ALU.add, op1=ALU.mult).then_inc(t1_done, 1)
                    dve.wait_ge(g0_ps, at(b, S0, s + 1))
                    dve.wait_ge(t1_done, at(b, S0, s + 1))
                    nc.vector.tensor_tensor(out=slot, in0=slot, in1=pa[:, 1, :], op=ALU.mult).then_inc(r0_done, 1)

                def add_y(b, k):
                    j, c = k // 2, k % 2
                    dve.wait_ge(red_done, at(b, GROUPS, 4 * k + 4))
                    if c == 0:
                        dve.wait_ge(xt_in[j], at(b, 16, 16))
                    nc.vector.tensor_tensor(out=xt[:, j, c, :], in0=y[:, :], in1=xt[:, j, c, :], op=ALU.add)\
                        .then_inc(y_free, 1)

                def add_down(b, j, c):
                    dve.wait_ge(down_ps, at(b, 4, 2 * j + c + 1))
                    dve.wait_ge(y_free, at(b, 4, 2 * j + c + 1))
                    if l1 and j == 0:
                        dve.wait_ge(out_done, at(m, 4, c + 1))
                    nc.vector.scalar_tensor_tensor(out=x2[:, c, j * BLK:(j + 1) * BLK], in0=acc[:, c, :],
                                                   scalar=sdown[:, 1:2], in1=xt[:, j, c, :],
                                                   op0=ALU.mult, op1=ALU.add).then_inc(x2_done, 1)

                def low_part1(j):
                    for c in range(KC):
                        cut = slice(j * BLK, (j + 1) * BLK)
                        dve.wait_ge(xh_done1, at(m, 4, 2 * j + c + 1))
                        nc.vector.scalar_tensor_tensor(out=xl1[:, c, cut], in0=pb[:, c, :], scalar=X_SCALE,
                                                       in1=xh1[:, c, cut], op0=ALU.mult, op1=ALU.subtract)\
                            .then_inc(xl_done1, 1)

                def moments1(j):
                    dve.wait_ge(x2_tok, at(m, 4, 2 * j + 2))
                    moments(1, x2tok, range(j * BT, (j + 1) * BT), stats1, at(m, 2, j + 1), agg1)

                def normalise1(j):
                    dve.wait_ge(rstd1, at(m, 2, j + 1))
                    normalise(1, x2tok, range(j * BT, (j + 1) * BT), xn_tok1)

                def q_minimum(n):
                    dve.wait_ge(q_ps, at(m, 4, n + 1))
                    if n >= 2:
                        dve.wait_ge(qf_done, at(m, 4, n - 1))
                    nc.vector.tensor_scalar(q_min[:, n % 2, :], pb[:, n % 2, :], cols[:, 2, n % 2:n % 2 + 1], 0.0,
                                            ALU.add, ALU.min).then_inc(qm_done, 1)

                def kv_bias(t):
                    dve.wait_ge(kv_ps, at(m, 8, t + 1))
                    if t >= 2:
                        dve.wait_ge(kv_acc, at(m, 8, t - 1))
                        dve.wait_ge(kf_done, at(m, 8, t - 1))
                    nc.vector.tensor_tensor(out=vx[:, t % 2, :, 0:P],
                                            in0=pb[:, t % 2, H:2 * H].rearrange("p (c m) -> p c m", c=KC),
                                            in1=bkv_sb[:, H:2 * H].rearrange("p (c m) -> p c m", c=KC), op=ALU.add)
                    nc.vector.tensor_tensor(out=k_all[:, 0, t % 2, :], in0=pb[:, t % 2, 0:H], in1=bkv_sb[:, 0:H],
                                            op=ALU.add).then_inc(kv_sb, 1)
                    dve.wait_ge(kv_sb, at(m, 8, t + 1))
                    nc.vector.tensor_scalar(k_all[:, 1, t % 2, :], k_all[:, 0, t % 2, :], 0.0, None, ALU.min)\
                        .then_inc(km_done, 1)

                def k_feature(t):
                    dve.wait_ge(ke_done, at(m, 8, t + 1))
                    if t >= 2:
                        dve.wait_ge(kv_acc, at(m, 8, t - 1))
                    nc.vector.scalar_tensor_tensor(out=kf[:, t % 2, :], in0=k_all[:, 0, t % 2, :], scalar=0.0,
                                                   in1=k_all[:, 1, t % 2, :], op0=ALU.max, op1=ALU.add)\
                        .then_inc(kf_done, 1)

                def head_blocks():
                    dve.wait_ge(kv_acc, at(m, 8, 8))
                    for c in range(KC):
                        nc.vector.tensor_tensor(out=kvx[:, c, 0:P], in0=acc[:, c, 0:P], in1=heads[:, :], op=ALU.mult)
                        last = nc.vector.tensor_copy(ksum[:, c:c + 1], acc[:, c, P:P + 1])
                    last.then_inc(ksum_done, 1)
                    dve.wait_ge(ksum_done, at(m, 1, 1))
                    for c in range(KC):
                        last = nc.vector.tensor_scalar(kvx[:, c, P:OW], head_of[:, :], ksum[:, c:c + 1], None, ALU.mult)
                    last.then_inc(kvx_done, 1)

                def divide(t):
                    r, half = t % 2, (t + 1) % 2
                    dve.wait_ge(o_ps, at(m, 8, t + 1))
                    bank = pb[:, half, 0:KC * OW].rearrange("p (c w) -> p c w", c=KC)
                    nc.vector.tensor_scalar(den[:, r, 0, :].rearrange("p (c h) -> p c h", c=KC), bank[:, :, P:OW],
                                            DEN_EPS, None, ALU.add).then_inc(den_done, 1)
                    dve.wait_ge(den_done, at(m, 16, 2 * t + 1))
                    nc.vector.reciprocal(den[:, r, 1, :], den[:, r, 0, :]).then_inc(den_done, 1)
                    dve.wait_ge(den_done, at(m, 16, 2 * t + 2))
                    for c in range(KC):
                        last = nc.vector.tensor_tensor(
                            out=otok[:, r, c * P:(c + 1) * P].rearrange("p (h e) -> p h e", e=DK),
                            in0=bank[:, c, 0:P].rearrange("p (h e) -> p h e", e=DK),
                            in1=den[:, r, 1, c * HPC:(c + 1) * HPC].unsqueeze(2).to_broadcast([P, HPC, DK]),
                            op=ALU.mult)
                    last.then_inc(otok_done, 1)

                def gate1(s):
                    rows = rows1(s)
                    slot = th1[0:rows, s % 2, :]
                    dve.wait_ge(th1_done, at(m, S1, s + 1))
                    dve.wait_ge(g1_ps, at(m, S1, s + 1))
                    nc.vector.scalar_tensor_tensor(out=slot, in0=slot, scalar=1.0, in1=pb[0:rows, 1, :],
                                                   op0=ALU.add, op1=ALU.mult).then_inc(r1_done, 1)

                def add_out(n):
                    j, c = n // KC, n % KC
                    cut = slice(j * BLK, (j + 1) * BLK)
                    dve.wait_ge(y2_ps, at(m, 4, n + 1))
                    nc.vector.scalar_tensor_tensor(out=xn1[:, c, cut], in0=pb[:, (n + 1) % 2, :],
                                                   scalar=cols[:, 3, c:c + 1], in1=x2[:, c, cut],
                                                   op0=ALU.add, op1=ALU.add).then_inc(out_done, 1)

                for g in range(GROUPS):
                    s1 = g - FFN1_G if l1 and 0 <= g - FFN1_G < S1 else None
                    if l0:
                        for j, f in FRONT.items():
                            if (j or more) and g == f + 2:
                                fronts[j][2](j)
                        unit(4 * g)
                        if g and g % 4 == 0:
                            add_y(b, g // 4 - 1)
                    if g == 0 and l1:
                        add_y(m, 3)
                    if l0:
                        gate0(g)
                    if l1:
                        for j in range(NJ):
                            if g == TOKENS_G[j] + 1:
                                moments1(j)
                    if l0:
                        unit(4 * g + 1)
                    if l1:
                        for j in range(NJ):
                            if g == TOKENS_G[j] + 1:
                                normalise1(j)
                            if g == TOKENS_G[j] + 2:
                                low_part1(j)
                        for t in range(2 * (g - KV_G - 1), 2 * (g - KV_G)):
                            if 0 <= t < NT:
                                k_feature(t)
                        if g == KV_G + 5:
                            head_blocks()
                        for n in ADD_OUT.get(g, ()):
                            add_out(n)
                    if s1 is not None:
                        gate1(s1)
                    if l0:
                        unit(4 * g + 2)
                    if l1:
                        for t in range(2 * (g - KV_G), 2 * (g - KV_G) + 2):
                            if 0 <= t < NT:
                                kv_bias(t)
                        for n in range(2 * (g - Q_G), 2 * (g - Q_G) + 2):
                            if 0 <= n < 4:
                                q_minimum(n)
                        if 0 <= g - ATTEND_G < NT // 2:
                            divide(2 * (g - ATTEND_G))
                    if l0:
                        unit(4 * g + 3)
                    if l1 and 0 <= g - ATTEND_G < NT // 2:
                        divide(2 * (g - ATTEND_G) + 1)
                    if l0:
                        for j, f in FRONT.items():
                            if (j or more) and g == f:
                                fronts[j][0](j)
                                fronts[j][1](j)
                        if g == GROUPS - 1:
                            add_down(b, 0, 0)
                            add_down(b, 0, 1)
                    if l1 and g < KC:
                        add_down(m, 1, g)
                if l1:
                    add_out(2)
                    add_out(3)
                    dve.wait_ge(out_done, at(m, 4, 4))

            moments0, normalise0, low_part0 = front_steps((0, 0))
            moments0(0)
            normalise0(0)
            low_part0(0)
            setup()
            thresholds()
            quantise(0, flat(q_up), raw0[:, 0, :], KC * F0, UP_Q)
            quantise(1, flat(q_gate), raw0[:, 1, :], KC * F0, UP_Q)
            quantise(2, flat(q_down), raw0[:, 2, :], KC * F0, 1.0)
            quantise(3, flat(q_w1), raw1[:, 0, 0:KC * F1], KC * F1, UP_Q)
            quantise(4, flat(q_w2), raw1[:, 1, 0:KC * F1], KC * F1, W2_Q)
            quantise(5, flat(q_w3), raw1[:, 2, :], RAW1, W3_Q)
            body(0, True, False, True, first=True)
            with dve.Fori(1, NBATCH - 1) as i:
                body(i, True, True, True)
            body(NBATCH - 1, True, True, False)
            body(NBATCH, False, True, False)

        @block.tensor
        def _(pe):
            mm = nc.tensor.matmul

            def wide(bank, w, f, rows, high, low, done):
                n = 0
                for k in range(KC):
                    for part in (high, low):
                        last = mm(bank[0:rows, :], w[:, k, f * P:f * P + rows], part[k],
                                  start=(n == 0), stop=(n == 2 * KC - 1))
                        n += 1
                last.then_inc(done, 1)

            def front_steps(b, steps=None):
                def to_channels0(j, g=None):
                    pe.wait_ge(xn_tok0, at(b, 8, 4 * j + 4))
                    if steps:
                        pe.wait_ge(r0_done, at(steps, S0, g + 1))
                    for c in range(KC):
                        for t in range(BT):
                            last = nc.tensor.transpose(pa[:, c, t * P:(t + 1) * P],
                                                       xtok[:, t, c * P:(c + 1) * P], ident[:, :])
                        last.then_inc(xnt_ps0, 1)

                def low(j, g=None):
                    pe.wait_ge(xl_done0, at(b, 4, 2 * j + 2))
                    if steps:
                        pe.wait_ge(t1_done, at(steps, S0, g + 1))
                    for k in range(KC):
                        last = mm(pa[0:RANK + 2 * NS, 0, :], win_sb[:, k, :], xn0[:, j, k, :],
                                  start=(k == 0), stop=(k == KC - 1))
                    last.then_inc(low_ps, 1)

                def pre(j, g=None):
                    pe.wait_ge(low_sb, at(b, 2, j + 1))
                    if steps:
                        pe.wait_ge(r0_done, at(steps, S0, g + 1))
                    for c in range(KC):
                        mm(pa[:, c, :], wdt_sb[:, c * P:(c + 1) * P], lbc[0:RANK, :], start=True, stop=True)\
                            .then_inc(pre_ps, 1)

                return to_channels0, low, pre

            def body(i, l0, l1, more, first=False):
                b, m = (i, 0), (i, 1)
                fronts = {1: front_steps(b, b), 0: front_steps((i, -1), b)}

                def gated0(s):
                    j, f = s // FT0, s % FT0
                    high, low_ = [xh0[:, j, k, :] for k in range(KC)], [xl0[:, j, k, :] for k in range(KC)]
                    if s == 0 and first:
                        pe.wait_ge(pre_free, 2)
                    elif s == FRONT[1] + 2:
                        pe.wait_ge(xl_done0, at(b, 4, 4))
                    elif s == FRONT[1] + 3:
                        pe.wait_ge(low_sb, at(b, 2, 2))
                    elif s == FRONT[1] + 4:
                        pe.wait_ge(pre_free, at(b, 4, 4))
                    elif s == FRONT[0] + 2 and more:
                        pe.wait_ge(xl_done0, at(b, 4, 6))
                    elif s == FRONT[0] + 3 and more:
                        pe.wait_ge(low_sb, at(b, 2, 3))
                    elif s == FRONT[0] + 4 and more:
                        pe.wait_ge(pre_free, at(b, 4, 6))
                    else:
                        pe.wait_ge(t1_done, at(b, S0, s))
                    wide(pa[:, 0, :], q_up, f, P, high, low_, u0_ps)
                    wait(pe, r0_done, at(b, S0, s))
                    wide(pa[:, 1, :], q_gate, f, P, high, low_, g0_ps)

                def skip(k):
                    if k or not first:
                        wait(pe, y_free, at(b, 4, k))
                    for q in range(NQ):
                        mm(y[q * CB:(q + 1) * CB, :], diag_d[:, k % KC, q * CB:(q + 1) * CB], xn0[:, k // KC, k % KC, :],
                           start=True, stop=False, tile_position=(0, q * CB))

                def reduce(b, g):
                    pe.wait_ge(prod_done, at(b, UNITS, 4 * g + 4))
                    for q in range(NQ):
                        last = mm(y[q * CB:(q + 1) * CB, :], reduce_w[:, :], prod[:, (4 * g + q) % PROD, :],
                                  start=False, stop=(g % 4 == 3), tile_position=(0, q * CB))
                    last.then_inc(red_done, 1)

                def down0(b, j, c):
                    if c == 0:
                        pe.wait_ge(lo0_done, at(b, S0, (j + 1) * FT0))
                    if j:
                        pe.wait_ge(x2_done, at(b, 4, c + 1))
                    elif l1:
                        pe.wait_ge(kvx_done, at(m, 1, 1))
                    for f in range(FT0):
                        for w in range(2):
                            last = mm(acc[:, c, :], q_down[:, f, c * P:(c + 1) * P],
                                      hid0[:, slot0(j * FT0 + f), w, :],
                                      start=(f == 0 and w == 0), stop=(f == FT0 - 1 and w == 1))
                    last.then_inc(down_ps, 1)

                def to_tokens(p):
                    pe.wait_ge(x2_done, at(m, 4, 2 if p < 2 else 4))
                    if p == 0:
                        pe.wait_ge(y_free, at(m, 4, 4))
                    if p >= 2:
                        pe.wait_ge(xl_done1, at(m, 4, p - 1))
                    for t in range(2):
                        for c in range(KC):
                            tok = (2 * p + t) * P
                            last = nc.tensor.transpose(pb[:, p % 2, (t * KC + c) * P:(t * KC + c + 1) * P],
                                                       x2[:, c, tok:tok + P], ident[:, :])
                    last.then_inc(x2_ps, 1)

                def to_channels1(j):
                    pe.wait_ge(xn_tok1, at(m, 8, 4 * j + 4))
                    for c in range(KC):
                        if j:
                            pe.wait_ge(kv_sb, at(m, 8, c + 1))
                        for t in range(BT):
                            last = nc.tensor.transpose(pb[:, c, t * P:(t + 1) * P],
                                                       x2tok[:, BT * j + t, c * P:(c + 1) * P], ident[:, :])
                        last.then_inc(xnt_ps1, 1)

                def bank_of_step(bank, g):
                    pe.wait_ge((th1_done, r1_done)[bank], at(m, S1, g - FFN1_G + 1))

                def q_proj(n):
                    c, j = n % 2, n // 2
                    bank_of_step(n % 2, Q_G + n // 2)
                    for k in range(KC):
                        last = mm(pb[:, n % 2, :], wq_sb[:, k, c * P:(c + 1) * P],
                                  xn1[:, k, j * BLK:(j + 1) * BLK], start=(k == 0), stop=(k == KC - 1))
                    last.then_inc(q_ps, 1)

                def kv_proj(t):
                    bank_of_step(t % 2, KV_G + t // 2)
                    for k in range(KC):
                        last = mm(pb[:, t % 2, :], xn1[:, k, t * P:(t + 1) * P], wkv_sb[:, k, :],
                                  start=(k == 0), stop=(k == KC - 1))
                    last.then_inc(kv_ps, 1)

                def kv_sum(t):
                    pe.wait_ge(kf_done, at(m, 8, t + 1))
                    for c in range(KC):
                        last = mm(acc[:, c, 0:P + 1], kf[:, t % 2, c * P:(c + 1) * P], vx[:, t % 2, c, :],
                                  start=(t == 0), stop=(t == NT - 1))
                    last.then_inc(kv_acc, 1)

                def gated1(s):
                    j, f = s // FT1, s % FT1
                    cut = slice(j * BLK, (j + 1) * BLK)
                    high, low_ = [xh1[:, k, cut] for k in range(KC)], [xl1[:, k, cut] for k in range(KC)]
                    g = s + FFN1_G
                    for bank, w, scale_done in ((0, q_w1, u1_ps), (1, q_w2, g1_ps)):
                        if s == 0:
                            pe.wait_ge(x2_tok, at(m, 4, 3 + bank))
                        elif s == 1:
                            pe.wait_ge(xl_done1, at(m, 4, 3 + bank))
                        elif g <= Q_G:
                            pe.wait_ge(kv_sb, at(m, 8, 2 * (g - KV_G) - 1 + bank))
                        elif g <= ATTEND_G:
                            pe.wait_ge(qe_done, at(m, 4, 2 * (g - Q_G) - 1 + bank))
                        elif g <= ATTEND_G + 4:
                            pe.wait_ge(otok_done, at(m, 8, 2 * (g - ATTEND_G) - bank))
                        elif bank == 0:
                            pe.wait_ge(ot_done, at(m, 4, 4))
                        else:
                            pe.wait_ge(out_done, at(m, 4, 1))
                        wide(pb[:, bank, :], w, f, rows1(s), high, low_, scale_done)

                def attend(t):
                    if t == 0:
                        pe.wait_ge(kvx_done, at(m, 1, 1))
                        pe.wait_ge(qf_done, at(m, 4, 4))
                    if t % 2 == 0:
                        pe.wait_ge(r1_done, at(m, S1, ATTEND_G + t // 2 - FFN1_G + 1))
                    elif t == 1:
                        pe.wait_ge(th1_done, at(m, S1, ATTEND_G - FFN1_G + 1))
                    else:
                        pe.wait_ge(ot_done, at(m, 4, t // 2))
                    for c in range(KC):
                        last = mm(pb[:, (t + 1) % 2, c * OW:(c + 1) * OW], qf[:, c, t * P:(t + 1) * P], kvx[:, c, :],
                                  start=True, stop=True)
                    last.then_inc(o_ps, 1)

                def back(p):
                    pe.wait_ge(otok_done, at(m, 8, 2 * p + 2))
                    pe.wait_ge(th1_done, at(m, S1, ATTEND_G + 1 + p - FFN1_G + 1))
                    for c in range(KC):
                        for r in range(2):
                            last = nc.tensor.transpose(pb[:, 0, (c * 2 + r) * P:(c * 2 + r + 1) * P],
                                                       otok[:, r, c * P:(c + 1) * P], ident[:, :])
                    last.then_inc(ot_ps, 1)

                def outputs1(n):
                    j, c = n // KC, n % KC
                    bank, cut = pb[:, (n + 1) % 2, :], slice(j * BLK, (j + 1) * BLK)
                    if c == 0:
                        pe.wait_ge(lo1_done, at(m, S1, (j + 1) * FT1))
                        pe.wait_ge(ot_done, at(m, 4, 2 * j + 2))
                    if n == 0:
                        pe.wait_ge(r1_done, at(m, S1, S1 - 1))
                    elif n == 1:
                        pe.wait_ge(th1_done, at(m, S1, S1))
                    elif n == 2:
                        pe.wait_ge(r1_done, at(m, S1, S1))
                    else:
                        pe.wait_ge(out_done, at(m, 4, 2))
                    for k in range(KC):
                        mm(bank, wo_sb[:, k, c * P:(c + 1) * P], qf[:, k, cut], start=(k == 0), stop=False)
                    for f in range(FT1):
                        rows = rows1(f)
                        for w in range(2):
                            last = mm(bank, q_w3[0:rows, f, c * P:(c + 1) * P],
                                      hid1[0:rows, j * FT1 + f, w, :], start=False, stop=(f == FT1 - 1 and w == 1))
                    last.then_inc(y2_ps, 1)

                for g in range(GROUPS):
                    s1 = g - FFN1_G if l1 and 0 <= g - FFN1_G < S1 else None
                    if l0:
                        gated0(g)
                        if g:
                            if (g - 1) % 4 == 0:
                                skip((g - 1) // 4)
                            reduce(b, g - 1)
                    if g == 0 and l1:
                        reduce(m, GROUPS - 1)
                    if l1 and g < KC:
                        down0(m, 1, g)
                    if l1:
                        if g == TOKENS_G[0]:
                            to_tokens(0)
                            to_tokens(1)
                        for t in range(2 * (g - KV_G - 1), 2 * (g - KV_G)):
                            if 0 <= t < NT:
                                kv_sum(t)
                    if s1 is not None:
                        gated1(s1)
                    if l1:
                        for t in range(2 * (g - KV_G), 2 * (g - KV_G) + 2):
                            if 0 <= t < NT:
                                kv_proj(t)
                        for n in range(2 * (g - Q_G), 2 * (g - Q_G) + 2):
                            if 0 <= n < 4:
                                q_proj(n)
                        if 0 <= g - ATTEND_G - 1 < NT // 2:
                            back(g - ATTEND_G - 1)
                        if 0 <= g - ATTEND_G < NT // 2:
                            attend(2 * (g - ATTEND_G))
                            attend(2 * (g - ATTEND_G) + 1)
                        for n in OUT_GROUPS.get(g, ()):
                            outputs1(n)
                    if l0:
                        if g - DOWN_G in (0, 1):
                            down0(b, 0, g - DOWN_G)
                        for j, f in FRONT.items():
                            to_channels0, low, pre = fronts[j]
                            if (j or more) and g == f + 1:
                                to_channels0(j, g)
                            if (j or more) and g == f + 2:
                                low(j, g)
                            if (j or more) and g == f + 3:
                                pre(j, g)
                    if l1:
                        for j in range(NJ):
                            if g == TOKENS_G[j] + 1:
                                to_channels1(j)
                        if g == TOKENS_G[1]:
                            to_tokens(2)
                            to_tokens(3)

            to_channels0, low, pre = front_steps((0, 0))
            pe.wait_ge(w_small, 11 * 16)
            to_channels0(0)
            low(0)
            pre(0)
            pe.wait_ge(const_set, 1)
            pe.wait_ge(abs_done, 6)
            mm(y[:, 0:6], ones, scale_sb[:, 0, :], start=True, stop=True).then_inc(sums_ps, 1)
            pe.wait_ge(quant, 3)
            pe.wait_ge(setup_dve, 2)
            pe.wait_ge(w_attn, 4 * 16)
            body(0, True, False, True, first=True)
            with pe.Fori(1, NBATCH - 1) as i:
                body(i, True, True, True)
            body(NBATCH - 1, True, True, False)
            body(NBATCH, False, True, False)


def kernel(**inputs):
    import numpy as np
    import concourse.bacc as bacc
    from concourse.bass_utils import run_bass_kernel_spmd

    a = {k: np.asarray(v) for k, v in inputs.items()}
    put = np.ascontiguousarray
    x = a["L0_attn_input"]
    chan, row = np.arange(P), np.arange(P)
    arrays = {
        "x_tok": put(x),
        "x_cm": put(x.transpose(0, 2, 1)),
        "w_in": put(np.concatenate([a["L0_attn_W_dt_in"], a["L0_attn_W_B"], a["L0_attn_W_C"]]).T),
        "w_dt_out": put(a["L0_attn_W_dt_out"].T),
        "b_dt": put(a["L0_attn_b_dt_out"]),
        "d_skip": put(a["L0_attn_D"]),
        "a_log": put(a["L0_attn_A_log"].reshape(KC * NQ, CB, NSB, SB).transpose(1, 3, 0, 2).reshape(P, -1)),
        "w_up": put(a["L0_ffn_W_up"].T), "w_gate": put(a["L0_ffn_W_gate"].T), "w_down": put(a["L0_ffn_W_down"].T),
        "wq": put(a["L1_attn_wq"].T), "bq": put(a["L1_attn_bq"]),
        "wkv": put(np.concatenate([a["L1_attn_wk"], a["L1_attn_wv"]]).T),
        "bkv": put(np.concatenate([a["L1_attn_bk"], a["L1_attn_bv"]])),
        "wo": put(a["L1_attn_wo"].T), "bo": put(a["L1_attn_bo"]),
        "w1": put(a["L1_ffn_w1"].T), "w2": put(a["L1_ffn_w2"].T), "w3": put(a["L1_ffn_w3"].T),
        "ident": np.eye(P, dtype=np.float32),
        "reduce": put((chan[:, None] // SB == np.arange(CB)[None, :]).astype(np.float32)),
        "heads": put((chan[:, None] // DK == row[None, :] // DK).astype(np.float32)),
        "head_of": put((chan[:, None] // DK == np.arange(HPC)[None, :]).astype(np.float32)),
    }
    nc = bacc.Bacc("TRN2", target_bir_lowering=False, num_devices=1, dynamic_dma_scratch_size=1024)
    args = [nc.dram_tensor(f"in_{k}", v.shape, mybir.dt.from_np(v.dtype), kind="ExternalInput").ap()
            for k, v in arrays.items()]
    out = nc.dram_tensor("out_cm", (NBATCH, H, T), mybir.dt.float32, kind="ExternalOutput").ap()
    two_layer_kernel(nc, *args, out)
    r = run_bass_kernel_spmd(nc, [{f"in_{k}": v for k, v in arrays.items()}], core_ids=[0])
    return np.ascontiguousarray(r.results[0]["out_cm"].transpose(0, 2, 1))
```

```python
import concourse.bass as bass
from concourse import mybir
from contextlib import ExitStack

P = 128
NBATCH, T, H = 4, 1024, 256
BLK = 512
NJ = T // BLK
NT = T // P
KC = H // P
NS, RANK = 16, 64
CB, NQ, SB = 32, 4, 4
NSB = NS // SB
F0, F1 = 1024, 704
FT0, FT1 = F0 // P, -(-F1 // P)
F1_LAST = F1 - (FT1 - 1) * P
HEADS, DK = 16, 16
HPC = HEADS // KC
OW = P + HPC
LN_EPS, Q_EPS, DEN_EPS = 1e-5, 1e-8, 1e-8

X_SCALE = 2.0 ** 11
UP_Q = 2.0 ** -12
W2_Q = 2.0 ** -5
W3_Q = 2.0 ** -7

S0, S1 = NJ * FT0, NJ * FT1
GROUPS = NJ * KC * NSB
UPB = KC * NSB * NQ
UNITS = NJ * UPB
BT = BLK // P
HID0 = 11
RING = 3
PROD = 6
LEAD = 2
RAW1 = FT1 * H

FRONT = {1: 0, 0: 8}
TOKENS_G = (0, 2)
FFN1_G, KV_G, Q_G = 2, 3, 7
ATTEND_G = 9
DOWN_G = 9
OUT_GROUPS = {13: (0,), 14: (1, 2), 15: (3,)}
ADD_OUT = {14: (0,), 15: (1, 2)}


def at(batch, per_batch, n):
    i, back = batch
    return i * per_batch + (n - back * per_batch)


def slot0(s):
    return s if s < HID0 else s - FT0


def user_before(u, ring):
    if u >= ring:
        return u - ring
    return max(v for v in range(UNITS) if v % ring == u) - UNITS


def wait(engine, semaphore, count):
    if not isinstance(count, int) or count > 0:
        engine.wait_ge(semaphore, count)


def two_layer_kernel(nc, x_tok, x_cm, w_in, w_dt_out, b_dt, d_skip, a_log, w_up, w_gate, w_down,
                     wq, bq, wkv, bkv, wo, bo, w1, w2, w3, ident_in, reduce_in, heads_in, head_of_in, out):
    f32, f16 = mybir.dt.float32, mybir.dt.float16
    ALU, ACT = mybir.AluOpType, mybir.ActivationFunctionType

    with ExitStack() as ctx:
        def sb(name, shape, dt=f32):
            return ctx.enter_context(nc.sbuf_tensor(name, shape, dt))

        def ps(name, shape):
            return ctx.enter_context(nc.psum_tensor(name, shape, f32))

        def sem(name):
            return ctx.enter_context(nc.semaphore(name))

        q_up = sb("q_up", [P, KC, F0], f16)
        q_gate = sb("q_gate", [P, KC, F0], f16)
        q_down = sb("q_down", [P, FT0, H], f16)
        q_w1 = sb("q_w1", [P, KC, F1], f16)
        q_w2 = sb("q_w2", [P, KC, F1], f16)
        q_w3 = sb("q_w3", [P, FT1, H], f16)
        win_sb = sb("win_sb", [P, KC, RANK + 2 * NS])
        wdt_sb = sb("wdt_sb", [RANK, H])
        wq_sb = sb("wq_sb", [P, KC, H])
        wkv_sb = sb("wkv_sb", [P, KC, 2 * H])
        wo_sb = sb("wo_sb", [P, KC, H])
        bkv_sb = sb("bkv_sb", [P, 2 * H])
        cols = sb("cols", [P, 5, KC])
        a_neg = sb("a_neg", [P, KC * NQ * NSB])
        ident = sb("ident", [P, P])
        reduce_w = sb("reduce_w", [P, CB])
        diag_d = sb("diag_d", [P, KC, P])
        heads = sb("heads", [P, P])
        head_of = sb("head_of", [P, HPC])
        neg_half = sb("neg_half", [P, NT])
        eps = sb("eps", [P, NT])
        spare = sb("spare", [P, 2])
        scale_sb = sb("scale_sb", [P, 5, 6])
        sdown = sb("sdown", [P, 2])

        xtok = sb("xtok", [P, BT, H])
        xt = sb("xt", [P, NJ, KC, BLK])
        xn0 = sb("xn0", [P, NJ, KC, BLK])
        xh0 = sb("xh0", [P, NJ, KC, BLK], f16)
        xl0 = sb("xl0", [P, NJ, KC, BLK], f16)
        lbc = sb("lbc", [RANK + 2 * NS, BLK])
        dt_sb = sb("dt_sb", [P, KC, BLK])
        dtu = sb("dtu", [P, KC, BLK])
        bc = sb("bc", [P, 2, NSB, BLK])
        dtb = sb("dtb", [P, 2, NQ, BLK])
        a_ring = sb("a_ring", [P, RING, BLK])
        b_ring = sb("b_ring", [P, RING, BLK])
        prod = sb("prod", [P, PROD, BLK])
        carry = sb("carry", [P, UPB])
        th0 = sb("th0", [P, 2, BLK])
        hid0 = sb("hid0", [P, HID0, 2, BLK], f16)
        x2 = sb("x2", [P, KC, T])
        wide1 = sb("wide1", [P, 3 * KC * T])
        xn1 = wide1[:, 0:KC * T].rearrange("p (c t) -> p c t", c=KC)
        qf = wide1[:, KC * T:2 * KC * T].rearrange("p (c t) -> p c t", c=KC)
        parts1 = wide1[:, 2 * KC * T:3 * KC * T].bitcast(f16).rearrange("p (w c t) -> p w c t", w=2, c=KC)
        xh1, xl1 = parts1[:, 0], parts1[:, 1]
        hid1_raw = sb("hid1_raw", [P, S1 * BLK])
        hid1 = hid1_raw[:, :].bitcast(f16).rearrange("p (s w t) -> p s w t", s=S1, w=2)
        x2tok = hid1_raw[:, 0:NT * H].rearrange("p (t h) -> p t h", h=H)
        th1 = sb("th1", [P, 2, BLK])
        ones = th1[:, 0, 0:P]
        q_min = sb("q_min", [P, 2, BLK])
        k_all = qf[:, 0, :].rearrange("p (w r t) -> p w r t", w=2, r=2)
        kf = q_min[:, 0, :].rearrange("p (r t) -> p r t", r=2)
        otok = q_min[:, 1, :].rearrange("p (r t) -> p r t", r=2)
        den = sb("den", [P, 2, 2, HEADS])
        ksum = sb("ksum", [P, KC])
        vx = sb("vx", [P, 2, KC, P + 1])
        kvx = sb("kvx", [P, KC, OW])
        stats = sb("stats", [P, NT, 6])
        mv = [sb(f"mv{l}", [P, NT, 2]) for l in range(2)]
        rstd = [sb(f"rstd{l}", [P, 2, NT]) for l in range(2)]
        raw0 = hid1_raw[:, 0:3 * KC * F0].rearrange("p (w n) -> p w n", w=3)
        raw1 = wide1[:, 0:3 * RAW1].rearrange("p (w n) -> p w n", w=3)
        hid0_flat = hid0[:, :, :, :].rearrange("p s w t -> p (s w t)")
        cmp_lo, cmp_hi = hid0_flat[:, 0:KC * F0], hid0_flat[:, KC * F0:2 * KC * F0]
        junk = x2[:, :, :].rearrange("p c t -> p (c t)")

        pa = ps("pa", [P, 2, BLK])
        pf = ps("pf", [P, BLK])
        pb = ps("pb", [P, 2, BLK])
        acc = ps("acc", [P, 2, BLK])
        y = ps("y", [P, BLK])

        w_small = sem("w_small"); w_raw0 = sem("w_raw0"); w_raw1 = sem("w_raw1"); w_attn = sem("w_attn")
        raw_tail = sem("raw_tail"); const_set = sem("const_set"); abs_done = sem("abs_done")
        sums_ps = sem("sums_ps"); setup_dve = sem("setup_dve"); setup_self = sem("setup_self")
        quant = sem("quant"); aneg_done = sem("aneg_done")
        xtok_in = sem("xtok_in")
        xt_in = [sem(f"xt_in{j}") for j in range(NJ)]
        stats0 = sem("stats0"); agg0 = sem("agg0"); rstd0 = sem("rstd0")
        xn_tok0 = sem("xn_tok0")
        xnt_ps0 = sem("xnt_ps0")
        xh_done0 = sem("xh_done0")
        xl_done0 = sem("xl_done0")
        low_ps = sem("low_ps"); low_sb = sem("low_sb")
        pre_ps = sem("pre_ps"); pre_free = sem("pre_free")
        sp_abs = sem("sp_abs"); sp_exp = sem("sp_exp"); sp_parts = sem("sp_parts")
        dt_sum = sem("dt_sum"); dt_done = sem("dt_done")
        bc_dram = sem("bc_dram")
        bc_in = [sem(f"bc_in{n}") for n in range(NSB)]
        dtb_in = [sem(f"dtb_in{n}") for n in range(NQ)]
        a_done = sem("a_done"); b_done = sem("b_done"); scan_done = sem("scan_done"); prod_done = sem("prod_done")
        red_done = sem("red_done")
        y_free = sem("y_free")
        u0_ps = sem("u0_ps"); g0_ps = sem("g0_ps"); th0_done = sem("th0_done"); t1_done = sem("t1_done")
        r0_done = sem("r0_done"); hi0_done = sem("hi0_done"); lo0_done = sem("lo0_done")
        down_ps = sem("down_ps"); x2_done = sem("x2_done")
        x2_ps = sem("x2_ps"); x2_tok = sem("x2_tok")
        stats1 = sem("stats1"); agg1 = sem("agg1"); rstd1 = sem("rstd1")
        xn_tok1 = sem("xn_tok1")
        xnt_ps1 = sem("xnt_ps1"); xh_done1 = sem("xh_done1"); xl_done1 = sem("xl_done1")
        q_ps = sem("q_ps"); qm_done = sem("qm_done"); qe_done = sem("qe_done"); qf_done = sem("qf_done")
        q_read = sem("q_read")
        kv_ps = sem("kv_ps"); kv_sb = sem("kv_sb"); km_done = sem("km_done"); ke_done = sem("ke_done")
        kf_done = sem("kf_done"); kv_acc = sem("kv_acc")
        ksum_done = sem("ksum_done"); kvx_done = sem("kvx_done")
        u1_ps = sem("u1_ps"); g1_ps = sem("g1_ps"); th1_done = sem("th1_done")
        r1_done = sem("r1_done"); hi1_done = sem("hi1_done"); lo1_done = sem("lo1_done")
        o_ps = sem("o_ps"); den_done = sem("den_done"); otok_done = sem("otok_done")
        ot_ps = sem("ot_ps"); ot_done = sem("ot_done")
        y2_ps = sem("y2_ps"); out_done = sem("out_done")
        out_dram = [sem(f"out_dram{j}") for j in range(NJ)]
        rstd_self = sem("rstd_self")

        scratch = nc.dram_tensor("bc_scratch", (2 * NS, BLK), f32, kind="Internal").ap()
        block = ctx.enter_context(nc.Block())

        def step_of_unit(u):
            return u // UPB, u % UPB // (NSB * NQ), u // NQ % NSB, u % NQ

        def rows1(s):
            return F1_LAST if s % FT1 == FT1 - 1 else P

        @block.sync
        def _(sp):
            sp.dma_start(xtok[:, :, :], x_tok[0, 0:BLK].rearrange("(t p) h -> p t h", p=P)).then_inc(xtok_in, 16)
            for dst, src in ((ident[:, :], ident_in), (reduce_w[:, :], reduce_in), (heads[:, :], heads_in),
                             (head_of[:, :], head_of_in), (a_neg[:, :], a_log),
                             (win_sb[:, :, :], w_in.rearrange("(k p) m -> p k m", p=P)), (wdt_sb[:, :], w_dt_out),
                             (cols[:, 0, :], b_dt.rearrange("(k p) -> p k", p=P)),
                             (cols[:, 1, :], d_skip.rearrange("(k p) -> p k", p=P)),
                             (cols[:, 2, :], bq.rearrange("(k p) -> p k", p=P)),
                             (cols[:, 3, :], bo.rearrange("(k p) -> p k", p=P))):
                with nc.allow_non_contiguous_dma(reason="a few short columns"):
                    sp.dma_start(dst, src).then_inc(w_small, 16)
            for n, w in enumerate((w1, w2)):
                sp.dma_start(raw1[:, n, 0:KC * F1].rearrange("p (k m) -> p k m", k=KC),
                             w.rearrange("(k p) m -> p k m", p=P)).then_inc(w_raw1, 16)
            full = (FT1 - 1) * P
            sp.dma_start(raw1[:, 2, 0:(FT1 - 1) * H].rearrange("p (k m) -> p k m", k=FT1 - 1),
                         w3[0:full, :].rearrange("(k p) m -> p k m", p=P)).then_inc(w_raw1, 16)
            sp.dma_start(raw1[0:F1_LAST, 2, (FT1 - 1) * H:FT1 * H], w3[full:F1, :]).then_inc(w_raw1, 16)
            for dst, src in ((wq_sb, wq), (wkv_sb, wkv), (wo_sb, wo)):
                sp.dma_start(dst[:, :, :], src.rearrange("(k p) m -> p k m", p=P)).then_inc(w_attn, 16)
            sp.dma_start(bkv_sb[:, :], bkv.rearrange("(a n) -> a n", a=1).to_broadcast([P, 2 * H])).then_inc(w_attn, 16)

            def layer0(i, first, last):
                b = (i, 0)

                def count(per_batch, n):
                    return n if first else sp.to_reg(at(b, per_batch, n))

                def tokens(batch, j, transposed):
                    sp.wait_ge(xnt_ps0, transposed)
                    sp.dma_start(xtok[:, :, :],
                                 x_tok[batch, j * BLK:(j + 1) * BLK].rearrange("(t p) h -> p t h", p=P))\
                      .then_inc(xtok_in, 16)

                def stream(j):
                    sp.dma_start(xt[:, j, :, :],
                                 x_cm[i, :, j * BLK:(j + 1) * BLK].rearrange("(k p) t -> p k t", p=P))\
                      .then_inc(xt_in[j], 16)

                def states(j, nb):
                    if j or not first:
                        sp.wait_ge(b_done, bc_used[j][nb])
                        sp.wait_ge(prod_done, bc_used[j][nb])
                    if nb == 0:
                        sp.wait_ge(bc_dram, in_dram[j])
                    for w in range(2):
                        row = w * NS + nb * SB
                        if nb == NSB - 1 and w == 1 and j == 0 and not first:
                            sp.wait_ge(x2_done, moved[0])
                        sp.dma_start(bc[:, w, nb, :],
                                     scratch[row:row + SB, :].unsqueeze(0).to_broadcast([CB, SB, BLK]))\
                          .then_inc(bc_in[nb], 16)

                transposed, moved = [count(4, 2), count(4, 4)], [count(4, 2 * j - 2) for j in range(NJ)]
                low_ready, in_dram = [count(2, j + 1) for j in range(NJ)], [count(32, 16 * j + 16) for j in range(NJ)]
                steps = [count(4, k + 1) for k in range(NJ * KC)]
                scratch_read = [count(64, 32 * j) for j in range(NJ)]
                bc_used = [[count(UNITS, (j - 1) * UPB + (NSB + nb + 1) * NQ) for nb in range(NSB)] for j in range(NJ)]
                dtb_used = [[count(UNITS, k * 16 - NQ + q + 1) for q in range(NQ)] for k in range(NJ * KC)]
                for j in range(NJ):
                    if j or not first:
                        for nb in range(NSB):
                            sp.wait_ge(bc_in[nb], scratch_read[j])
                    if j == 0:
                        tokens(i, 1, transposed[0])
                    sp.wait_ge(low_sb, low_ready[j])
                    sp.dma_start(scratch, lbc[RANK:RANK + 2 * NS, :]).then_inc(bc_dram, 16)
                    if j == 1 and not last:
                        tokens(i + 1, 0, transposed[1])
                    for nb in range(NSB - 1):
                        states(j, nb)
                    for c in range(KC):
                        k = j * KC + c
                        sp.wait_ge(dt_done, steps[k])
                        for q in range(NQ):
                            if k or not first:
                                sp.wait_ge(a_done, dtb_used[k][q])
                                sp.wait_ge(b_done, dtb_used[k][q])
                            for w, src in enumerate((dt_sb, dtu)):
                                if q == NQ - 1 and w == 1 and k == 1 and not first:
                                    sp.wait_ge(x2_done, moved[1])
                                sp.dma_start(dtb[:, w, q, :],
                                             src[q * CB:(q + 1) * CB, c, :].unsqueeze(1).to_broadcast([CB, SB, BLK]))\
                                  .then_inc(dtb_in[q], 16)
                        if c == 0:
                            states(j, NSB - 1)
                        if k < NJ:
                            stream(k)

            layer0(0, True, False)
            with sp.Fori(1, NBATCH - 1) as i:
                layer0(i, False, False)
            layer0(NBATCH - 1, False, True)
            for j in range(NJ):
                sp.wait_ge(out_dram[j], NBATCH * 32)
            sp.wait_ge(bc_dram, NBATCH * 32)

        @block.scalar
        def _(act):
            for n, w in enumerate((w_up, w_gate, w_down)):
                act.dma_start(raw0[:, n, :].rearrange("p (k m) -> p k m", k=w.shape[0] // P),
                              w.rearrange("(k p) m -> p k m", p=P)).then_inc(w_raw0, 16)
            act.wait_ge(w_small, 11 * 16)
            nc.scalar.activation(a_neg[:, :], a_neg[:, :], ACT.Exp).then_inc(aneg_done, 1)

            def magnitudes(layer):
                if layer == 0:
                    act.wait_ge(w_raw0, 3 * 16)
                else:
                    act.wait_ge(w_raw1, 4 * 16)
                    act.wait_ge(raw_tail, 1)
                for n in range(3):
                    raw = (raw0, raw1)[layer]
                    m = (KC * F0, KC * F0, FT0 * H, KC * F1, KC * F1, RAW1)[3 * layer + n]
                    nc.scalar.activation(junk[:, 0:m], raw[:, n, 0:m], ACT.Abs,
                                         accum_out=scale_sb[:, 0, 3 * layer + n:3 * layer + n + 1])\
                        .then_inc(abs_done, 1)
                    act.wait_ge(abs_done, 3 * layer + n + 1)

            def front_steps(b, first=False):
                def parts0(j, c):
                    act.wait_ge(xnt_ps0, at(b, 4, 2 * j + c + 1))
                    nc.scalar.activation(xn0[:, j, c, :], pf[:, :], ACT.Copy)
                    nc.scalar.activation(xh0[:, j, c, :], pf[:, :], ACT.Copy, scale=X_SCALE).then_inc(xh_done0, 1)

                def low(j):
                    act.wait_ge(low_ps, at(b, 2, j + 1))
                    nc.scalar.activation(lbc[:, :], pf[0:RANK + 2 * NS, :], ACT.Copy).then_inc(low_sb, 1)

                def softplus_parts(j, c):
                    k = 2 * j + c
                    act.wait_ge(pre_ps, at(b, 4, k + 1))
                    if k or not first:
                        for q in range(NQ):
                            wait(act, dtb_in[q], at(b, 128, 64 * j))
                    nc.scalar.activation(dt_sb[:, c, :], pf[:, :], ACT.Abs, bias=cols[:, 0, c:c + 1])\
                        .then_inc(sp_abs, 1)
                    nc.scalar.activation(dtu[:, c, :], pf[:, :], ACT.Relu, bias=cols[:, 0, c:c + 1])\
                        .then_inc(pre_free, 1)

                def softplus_exp(j):
                    for c in range(KC):
                        act.wait_ge(sp_abs, at(b, 4, 2 * j + c + 1))
                        nc.scalar.activation(dt_sb[:, c, :], dt_sb[:, c, :], ACT.Exp, scale=-1.0).then_inc(sp_exp, 1)

                def softplus_ln(j):
                    for c in range(KC):
                        act.wait_ge(sp_exp, at(b, 4, 2 * j + c + 1))
                        nc.scalar.activation(dt_sb[:, c, :], dt_sb[:, c, :], ACT.Ln, bias=1.0).then_inc(sp_parts, 1)

                return parts0, low, softplus_parts, softplus_exp, softplus_ln

            def decay(b, u, first=False):
                j, c, nb, q = step_of_unit(u)
                act.wait_ge(dtb_in[q], at(b, 128, (j * KC + c + 1) * 32))
                if u >= RING or not first:
                    wait(act, scan_done, at(b, UNITS, user_before(u, RING) + 1))
                k = (c * NQ + q) * NSB + nb
                nc.scalar.activation(a_ring[:, u % RING, :], dtb[:, 0, q, :], ACT.Exp,
                                     scale=a_neg[:, k:k + 1]).then_inc(a_done, 1)

            def body(i, l0, l1, more, first=False):
                b, m = (i, 0), (i, 1)
                fronts = {1: front_steps(b), 0: front_steps((i, -1))}

                def decay_ahead(u):
                    if u + LEAD < UNITS:
                        decay(b, u + LEAD, first)
                    elif more:
                        decay((i, -1), u + LEAD - UNITS)

                def tanh0(b, s, first=False):
                    act.wait_ge(u0_ps, at(b, S0, s + 1))
                    if s >= 2 or not first:
                        wait(act, lo0_done, at(b, S0, s - 1))
                    nc.scalar.activation(th0[:, s % 2, :], pa[:, 0, :], ACT.Tanh, scale=scale_sb[:, 2, 0:1])\
                        .then_inc(th0_done, 1)

                def high0(s):
                    act.wait_ge(r0_done, at(b, S0, s + 1))
                    if s >= HID0 or not first:
                        act.wait_ge(down_ps, at(b, 4, 2 if s >= HID0 else 0 if s >= HID0 - FT0 else -2))
                    nc.scalar.activation(hid0[:, slot0(s), 0, :], th0[:, s % 2, :], ACT.Copy).then_inc(hi0_done, 1)

                def tokens1(p):
                    act.wait_ge(x2_ps, at(m, 4, p + 1))
                    nc.scalar.activation(x2tok[:, 2 * p:2 * p + 2, :],
                                         pb[:, p % 2, :].rearrange("p (t h) -> p t h", t=2), ACT.Copy)\
                        .then_inc(x2_tok, 1)

                def parts1_of(j):
                    for c in range(KC):
                        cut = slice(j * BLK, (j + 1) * BLK)
                        act.wait_ge(xnt_ps1, at(m, 4, 2 * j + c + 1))
                        nc.scalar.activation(xn1[:, c, cut], pb[:, c, :], ACT.Copy)
                        nc.scalar.activation(xh1[:, c, cut], pb[:, c, :], ACT.Copy, scale=X_SCALE)\
                            .then_inc(xh_done1, 1)

                def q_feature(n):
                    c, j = n % 2, n // 2
                    act.wait_ge(q_ps, at(m, 4, n + 1))
                    if n >= 2:
                        act.wait_ge(qf_done, at(m, 4, n - 1))
                    nc.scalar.activation(q_min[:, n % 2, :], pb[:, n % 2, :], ACT.Relu, scale=-1.0,
                                         bias=cols[:, 4, c:c + 1]).then_inc(qm_done, 1)
                    nc.scalar.activation(qf[:, c, j * BLK:(j + 1) * BLK], pb[:, n % 2, :], ACT.Relu,
                                         bias=cols[:, 2, c:c + 1]).then_inc(q_read, 1)
                    act.wait_ge(qm_done, at(m, 4, n + 1))
                    nc.scalar.activation(q_min[:, n % 2, :], q_min[:, n % 2, :], ACT.Exp, scale=-1.0)\
                        .then_inc(qe_done, 1)

                def k_feature(t):
                    act.wait_ge(kv_sb, at(m, 8, t + 1))
                    nc.scalar.activation(k_all[:, 1, t % 2, :], k_all[:, 0, t % 2, :], ACT.Relu, scale=-1.0)\
                        .then_inc(km_done, 1)
                    act.wait_ge(km_done, at(m, 8, t + 1))
                    nc.scalar.activation(k_all[:, 1, t % 2, :], k_all[:, 1, t % 2, :], ACT.Exp, scale=-1.0)\
                        .then_inc(ke_done, 1)

                pw = pb if l0 else pa

                def tanh1(s):
                    act.wait_ge(u1_ps, at(m, S1, s + 1))
                    if s >= 2:
                        act.wait_ge(lo1_done, at(m, S1, s - 1))
                    nc.scalar.activation(th1[0:rows1(s), s % 2, :], pw[0:rows1(s), 0, :], ACT.Tanh).then_inc(th1_done, 1)

                def high1(s):
                    act.wait_ge(r1_done, at(m, S1, s + 1))
                    nc.scalar.activation(hid1[0:rows1(s), s, 0, :], th1[0:rows1(s), s % 2, :], ACT.Copy)\
                        .then_inc(hi1_done, 1)

                def attended(p):
                    act.wait_ge(ot_ps, at(m, 4, p + 1))
                    nc.scalar.activation(qf[:, :, 2 * p * P:(2 * p + 2) * P],
                                         pb[:, 0, :].rearrange("p (c t) -> p c t", c=KC), ACT.Copy)\
                        .then_inc(ot_done, 1)

                def store(n):
                    j, c = n // KC, n % KC
                    act.wait_ge(out_done, at(m, 4, n + 1))
                    act.dma_start(out[m[0] - m[1], c * P:(c + 1) * P, j * BLK:(j + 1) * BLK],
                                  xn1[:, c, j * BLK:(j + 1) * BLK]).then_inc(out_dram[j], 16)

                for g in range(GROUPS):
                    s1 = g - FFN1_G if l1 and 0 <= g - FFN1_G < S1 else None
                    if l0:
                        if g == 0 and first:
                            tanh0(b, 0, first)
                        for j, f in FRONT.items():
                            if (j or more) and g - f - 2 in (0, 1):
                                fronts[j][0](j, g - f - 2)
                            if (j or more) and g == f + 4:
                                fronts[j][1](j)
                        decay_ahead(4 * g)
                    if l1:
                        if g == TOKENS_G[0]:
                            tokens1(0)
                            tokens1(1)
                        if g == TOKENS_G[1] + 1:
                            tokens1(2)
                            tokens1(3)
                        for j in range(NJ):
                            if g == TOKENS_G[j] + 2:
                                parts1_of(j)
                        for t in range(2 * (g - KV_G - 1), 2 * (g - KV_G)):
                            if 0 <= t < NT:
                                k_feature(t)
                    if l0:
                        decay_ahead(4 * g + 1)
                    if s1 is not None and s1:
                        tanh1(s1)
                    if l0:
                        high0(g)
                        decay_ahead(4 * g + 2)
                    if s1 is not None and s1:
                        high1(s1)
                    if l1 and 0 <= g - ATTEND_G - 1 < NT // 2:
                        attended(g - ATTEND_G - 1)
                    if l0:
                        for j, f in FRONT.items():
                            if (j or more) and g - f - 5 in (0, 1):
                                fronts[j][2](j, g - f - 5)
                            if (j or more) and g == f + 6:
                                fronts[j][3](j)
                        decay_ahead(4 * g + 3)
                    if l0:
                        if g + 1 < GROUPS:
                            tanh0(b, g + 1, first)
                        elif more:
                            tanh0((i, -1), 0)
                    if l1:
                        for n in range(2 * (g - Q_G), 2 * (g - Q_G) + 2):
                            if 0 <= n < 4:
                                q_feature(n)
                    if l0:
                        for j, f in FRONT.items():
                            if (j or more) and g == f + 6:
                                fronts[j][4](j)
                    if s1 == 0:
                        tanh1(0)
                        high1(0)
                    if l1:
                        for n in ADD_OUT.get(g, ()):
                            store(n)
                if l1:
                    store(3)
                    for j in range(NJ):
                        act.wait_ge(out_dram[j], at(m, 32, 32))

            parts0, low, softplus_parts, softplus_exp, softplus_ln = front_steps((0, 0), first=True)
            parts0(0, 0)
            parts0(0, 1)
            magnitudes(0)
            low(0)
            softplus_parts(0, 0)
            softplus_parts(0, 1)
            softplus_exp(0)
            softplus_ln(0)
            magnitudes(1)
            act.wait_ge(setup_dve, 2)
            for u in range(LEAD):
                decay((0, 0), u, first=True)
            body(0, True, False, True, first=True)
            with act.Fori(1, NBATCH - 1) as i:
                body(i, True, True, True)
            body(NBATCH - 1, True, True, False)
            body(NBATCH, False, True, False)

        @block.gpsimd
        def _(pool):
            nc.gpsimd.memset(raw1[F1_LAST:P, 2, (FT1 - 1) * H:FT1 * H], 0.0).then_inc(raw_tail, 1)
            pool.wait_ge(raw_tail, 1)
            nc.gpsimd.memset(neg_half[:, :], -0.5)
            nc.gpsimd.memset(eps[:, :], LN_EPS)
            nc.gpsimd.memset(vx[:, :, :, P:P + 1], 1.0)
            nc.gpsimd.memset(ones, 1.0).then_inc(const_set, 1)
            pool.wait_ge(const_set, 1)

            def front_steps(b, self_n):
                def power(l, tiles, ready, ready_n, done, self_n):
                    pool.wait_ge(ready, ready_n)
                    nc.gpsimd.tensor_tensor(out=rstd[l][:, 0, tiles], in0=mv[l][:, tiles, 1], in1=eps[:, tiles],
                                            op=ALU.add).then_inc(rstd_self, 1)
                    pool.wait_ge(rstd_self, self_n)
                    nc.gpsimd.tensor_tensor(out=rstd[l][:, 1, tiles], in0=rstd[l][:, 0, tiles],
                                            in1=neg_half[:, tiles], op=ALU.pow).then_inc(done, 1)

                def rstd_of0(j):
                    power(0, slice(j * BT, (j + 1) * BT), agg0, at(b, 2, j + 1), rstd0, self_n)

                def time_step(j):
                    for c in range(KC):
                        k = 2 * j + c
                        pool.wait_ge(sp_parts, at(b, 4, k + 1))
                        nc.gpsimd.tensor_tensor(out=dt_sb[:, c, :], in0=dt_sb[:, c, :], in1=dtu[:, c, :], op=ALU.add)\
                            .then_inc(dt_sum, 1)
                        pool.wait_ge(dt_sum, at(b, 4, k + 1))
                        nc.gpsimd.tensor_tensor(out=dtu[:, c, :], in0=dt_sb[:, c, :], in1=xn0[:, j, c, :], op=ALU.mult)\
                            .then_inc(dt_done, 1)

                return power, rstd_of0, time_step

            def into_state(b, u, first=False):
                j, c, nb, q = step_of_unit(u)
                pool.wait_ge(dtb_in[q], at(b, 128, (j * KC + c + 1) * 32))
                pool.wait_ge(bc_in[nb], at(b, 64, 32 * j + 32))
                if u >= RING or not first:
                    wait(pool, prod_done, at(b, UNITS, user_before(u, RING) + 1))
                nc.gpsimd.tensor_tensor(out=b_ring[:, u % RING, :], in0=dtb[:, 1, q, :], in1=bc[:, 0, nb, :],
                                        op=ALU.mult).then_inc(b_done, 1)

            def body(i, l0, l1, more, first=False):
                b, m = (i, 0), (i, 1)
                power, _, _ = front_steps(m, None)
                fronts = {1: front_steps(b, 2 if first else at(b, 4, 0)),
                          0: front_steps((i, -1), 3 if first else at(b, 4, 3))}

                def rstd_of1(j):
                    power(1, slice(j * BT, (j + 1) * BT), agg1, at(m, 2, j + 1), rstd1,
                          at(b, 4, j + 1 if l0 else j - 1))

                def into_state_ahead(u):
                    if u + LEAD < UNITS:
                        into_state(b, u + LEAD, first)
                    elif more:
                        into_state((i, -1), u + LEAD - UNITS)

                def q_sum(n):
                    c, j = n % 2, n // 2
                    pool.wait_ge(qe_done, at(m, 4, n + 1))
                    part = qf[:, c, j * BLK:(j + 1) * BLK]
                    nc.gpsimd.tensor_tensor(out=part, in0=part, in1=q_min[:, n % 2, :], op=ALU.add)\
                        .then_inc(qf_done, 1)

                def low0(b, s):
                    pool.wait_ge(hi0_done, at(b, S0, s + 1))
                    nc.gpsimd.tensor_tensor(out=hid0[:, slot0(s), 1, :], in0=th0[:, s % 2, :],
                                            in1=hid0[:, slot0(s), 0, :], op=ALU.subtract).then_inc(lo0_done, 1)

                def low1(s):
                    rows = rows1(s)
                    pool.wait_ge(hi1_done, at(m, S1, s + 1))
                    nc.gpsimd.tensor_tensor(out=hid1[0:rows, s, 1, :], in0=th1[0:rows, s % 2, :],
                                            in1=hid1[0:rows, s, 0, :], op=ALU.subtract).then_inc(lo1_done, 1)

                for g in range(GROUPS):
                    if l1 and 0 <= g - 1 - FFN1_G < S1:
                        low1(g - 1 - FFN1_G)
                    if l1:
                        for n in range(2 * (g - Q_G - 1), 2 * (g - Q_G)):
                            if 0 <= n < 4:
                                q_sum(n)
                    if l0:
                        into_state_ahead(4 * g)
                    if g == 0 and l1:
                        low0(m, S0 - 1)
                    if l1:
                        for j in range(NJ):
                            if g == TOKENS_G[j] + 1:
                                rstd_of1(j)
                    if l0:
                        into_state_ahead(4 * g + 1)
                        if g:
                            low0(b, g - 1)
                        into_state_ahead(4 * g + 2)
                    if l0:
                        into_state_ahead(4 * g + 3)
                        for j, f in FRONT.items():
                            _, rstd_of0, time_step = fronts[j]
                            if (j or more) and g == f:
                                rstd_of0(j)
                            if (j or more) and g == f + 6:
                                time_step(j)

            _, rstd_of0, time_step = front_steps((0, 0), 1)
            rstd_of0(0)
            time_step(0)
            for u in range(LEAD):
                into_state((0, 0), u, first=True)
            body(0, True, False, True, first=True)
            with pool.Fori(1, NBATCH - 1) as i:
                body(i, True, True, True)
            body(NBATCH - 1, True, True, False)
            body(NBATCH, False, True, False)

        @block.vector
        def _(dve):
            def moments(l, tok, tiles, stat_sem, stat_n, agg_sem):
                for t in tiles:
                    last = nc.vector.bn_stats(stats[:, t, :], tok[:, t % tok.shape[1], :])
                last.then_inc(stat_sem, 1)
                dve.wait_ge(stat_sem, stat_n)
                nc.vector.memset(spare[:, :], 0.0)
                for t in tiles:
                    last = nc.vector.bn_aggr(mv[l][:, t, :], stats[:, t, :])
                last.then_inc(agg_sem, 1)

            def normalise(l, tok, tiles, done):
                for t in tiles:
                    tile = tok[:, t % tok.shape[1], :]
                    nc.vector.tensor_scalar(tile, tile, mv[l][:, t, 0:1], rstd[l][:, 1, t:t + 1],
                                            ALU.subtract, ALU.mult).then_inc(done, 1)

            def setup():
                dve.wait_ge(w_small, 11 * 16)
                for c in range(KC):
                    nc.vector.tensor_scalar(diag_d[:, c, :], ident[:, :], cols[:, 1, c:c + 1], None, ALU.mult)
                nc.vector.tensor_scalar(cols[:, 4, :], cols[:, 2, :], -1.0, None, ALU.mult)
                dve.wait_ge(aneg_done, 1)
                nc.vector.tensor_scalar(a_neg[:, :], a_neg[:, :], -1.0, None, ALU.mult).then_inc(setup_dve, 1)

            chain = [0]

            def link(ins):
                chain[0] += 1
                ins.then_inc(setup_self, 1)
                dve.wait_ge(setup_self, chain[0])

            def thresholds(layer):
                dve.wait_ge(sums_ps, layer + 1)
                three = slice(3 * layer, 3 * layer + 3)
                link(nc.vector.tensor_scalar(scale_sb[:, 1, three], y[:, three], 1.0 / ((F0, F1)[layer] * H), None,
                                             ALU.mult))
                link(nc.vector.tensor_scalar(scale_sb[:, 2, three], scale_sb[:, 1, three], Q_EPS, None, ALU.add))
                nc.vector.tensor_scalar(scale_sb[:, 3, three], scale_sb[:, 2, three], 0.5, None, ALU.mult)
                link(nc.vector.tensor_scalar(scale_sb[:, 4, three], scale_sb[:, 2, three], -0.5, None, ALU.mult))
                if layer == 0:
                    link(nc.vector.tensor_tensor(out=sdown[:, 0:1], in0=scale_sb[:, 2, 0:1],
                                                 in1=scale_sb[:, 2, 1:2], op=ALU.mult))
                    nc.vector.scalar_tensor_tensor(out=sdown[:, 1:2], in0=sdown[:, 0:1], scalar=2.0,
                                                   in1=scale_sb[:, 2, 2:3], op0=ALU.mult, op1=ALU.mult)\
                        .then_inc(setup_dve, 1)

            def quantise(n, dst, src, size, q):
                nc.vector.tensor_scalar(cmp_lo[:, 0:size], src, scale_sb[:, 4, n:n + 1], q, ALU.is_lt, ALU.mult)
                link(nc.vector.tensor_scalar(cmp_hi[:, 0:size], src, scale_sb[:, 3, n:n + 1], q, ALU.is_gt, ALU.mult))
                nc.vector.tensor_tensor(out=dst, in0=cmp_hi[:, 0:size], in1=cmp_lo[:, 0:size], op=ALU.subtract)\
                    .then_inc(quant, 1)
                dve.wait_ge(quant, n + 1)

            def flat(w):
                return w[:, :, :].rearrange("p k m -> p (k m)")

            def front_steps(b):
                def moments0(j):
                    dve.wait_ge(xtok_in, at(b, 32, 16 * j + 16))
                    moments(0, xtok, range(j * BT, (j + 1) * BT), stats0, at(b, 2, j + 1), agg0)

                def normalise0(j):
                    dve.wait_ge(rstd0, at(b, 2, j + 1))
                    normalise(0, xtok, range(j * BT, (j + 1) * BT), xn_tok0)

                def low_part0(j, c):
                    dve.wait_ge(xh_done0, at(b, 4, 2 * j + c + 1))
                    nc.vector.scalar_tensor_tensor(out=xl0[:, j, c, :], in0=pf[:, :], scalar=X_SCALE,
                                                   in1=xh0[:, j, c, :], op0=ALU.mult, op1=ALU.subtract)\
                        .then_inc(xl_done0, 1)

                return moments0, normalise0, low_part0

            def body(i, l0, l1, more, first=False):
                b, m = (i, 0), (i, 1)
                fronts = {1: front_steps(b), 0: front_steps((i, -1))}

                def scan(u):
                    j, c, nb, q = step_of_unit(u)
                    v = u % UPB
                    dve.wait_ge(a_done, at(b, UNITS, u + 1))
                    dve.wait_ge(b_done, at(b, UNITS, u + 1))
                    slot = b_ring[:, u % RING, :]
                    nc.vector.tensor_tensor_scan(out=slot, data0=a_ring[:, u % RING, :], data1=slot,
                                                 initial=carry[:, v:v + 1] if j else 0.0,
                                                 op0=ALU.mult, op1=ALU.add).then_inc(scan_done, 1)

                def product(u):
                    j, c, nb, q = step_of_unit(u)
                    v = u % UPB
                    slot = b_ring[:, u % RING, :]
                    if u >= PROD or not first:
                        wait(dve, red_done, at(b, GROUPS, user_before(u, PROD) // 4 + 1))
                    dve.wait_ge(bc_in[nb], at(b, 64, 32 * j + 32))
                    dve.wait_ge(scan_done, at(b, UNITS, u + 1))
                    if j == 0:
                        nc.vector.tensor_copy(carry[:, v:v + 1], slot[:, BLK - 1:BLK])
                    nc.vector.tensor_tensor(out=prod[:, u % PROD, :], in0=slot, in1=bc[:, 1, nb, :],
                                            op=ALU.mult).then_inc(prod_done, 1)

                def unit(u):
                    scan(u)
                    if u:
                        product(u - 1)

                def gate0(s):
                    slot = th0[:, s % 2, :]
                    dve.wait_ge(th0_done, at(b, S0, s + 1))
                    nc.vector.scalar_tensor_tensor(out=slot, in0=slot, scalar=1.0, in1=pa[:, 0, :],
                                                   op0=ALU.add, op1=ALU.mult).then_inc(t1_done, 1)

                def times_gate0(s):
                    slot = th0[:, s % 2, :]
                    dve.wait_ge(g0_ps, at(b, S0, s + 1))
                    dve.wait_ge(t1_done, at(b, S0, s + 1))
                    nc.vector.tensor_tensor(out=slot, in0=slot, in1=pa[:, 1, :], op=ALU.mult).then_inc(r0_done, 1)

                def add_y(b, k):
                    j, c = k // 2, k % 2
                    dve.wait_ge(red_done, at(b, GROUPS, 4 * k + 4))
                    if c == 0:
                        dve.wait_ge(xt_in[j], at(b, 16, 16))
                    nc.vector.tensor_tensor(out=xt[:, j, c, :], in0=y[:, :], in1=xt[:, j, c, :], op=ALU.add)\
                        .then_inc(y_free, 1)

                def add_down(b, j, c):
                    dve.wait_ge(down_ps, at(b, 4, 2 * j + c + 1))
                    dve.wait_ge(y_free, at(b, 4, 2 * j + c + 1))
                    if l1 and j == 0:
                        dve.wait_ge(out_done, at(m, 4, c + 1))
                    nc.vector.scalar_tensor_tensor(out=x2[:, c, j * BLK:(j + 1) * BLK], in0=acc[:, c, :],
                                                   scalar=sdown[:, 1:2], in1=xt[:, j, c, :],
                                                   op0=ALU.mult, op1=ALU.add).then_inc(x2_done, 1)

                def low_part1(j):
                    for c in range(KC):
                        cut = slice(j * BLK, (j + 1) * BLK)
                        dve.wait_ge(xh_done1, at(m, 4, 2 * j + c + 1))
                        nc.vector.scalar_tensor_tensor(out=xl1[:, c, cut], in0=pb[:, c, :], scalar=X_SCALE,
                                                       in1=xh1[:, c, cut], op0=ALU.mult, op1=ALU.subtract)\
                            .then_inc(xl_done1, 1)

                def moments1(j):
                    dve.wait_ge(x2_tok, at(m, 4, 2 * j + 2))
                    moments(1, x2tok, range(j * BT, (j + 1) * BT), stats1, at(m, 2, j + 1), agg1)

                def normalise1(j):
                    dve.wait_ge(rstd1, at(m, 2, j + 1))
                    normalise(1, x2tok, range(j * BT, (j + 1) * BT), xn_tok1)

                def kv_bias(t):
                    dve.wait_ge(kv_ps, at(m, 8, t + 1))
                    if t >= 2:
                        dve.wait_ge(kv_acc, at(m, 8, t - 1))
                        dve.wait_ge(kf_done, at(m, 8, t - 1))
                    nc.vector.tensor_tensor(out=vx[:, t % 2, :, 0:P],
                                            in0=pb[:, t % 2, H:2 * H].rearrange("p (c m) -> p c m", c=KC),
                                            in1=bkv_sb[:, H:2 * H].rearrange("p (c m) -> p c m", c=KC), op=ALU.add)
                    nc.vector.tensor_tensor(out=k_all[:, 0, t % 2, :], in0=pb[:, t % 2, 0:H], in1=bkv_sb[:, 0:H],
                                            op=ALU.add).then_inc(kv_sb, 1)

                def k_feature(t):
                    dve.wait_ge(ke_done, at(m, 8, t + 1))
                    if t >= 2:
                        dve.wait_ge(kv_acc, at(m, 8, t - 1))
                    nc.vector.scalar_tensor_tensor(out=kf[:, t % 2, :], in0=k_all[:, 0, t % 2, :], scalar=0.0,
                                                   in1=k_all[:, 1, t % 2, :], op0=ALU.max, op1=ALU.add)\
                        .then_inc(kf_done, 1)

                def head_blocks():
                    dve.wait_ge(kv_acc, at(m, 8, 8))
                    for c in range(KC):
                        nc.vector.tensor_tensor(out=kvx[:, c, 0:P], in0=acc[:, c, 0:P], in1=heads[:, :], op=ALU.mult)
                        last = nc.vector.tensor_copy(ksum[:, c:c + 1], acc[:, c, P:P + 1])
                    last.then_inc(ksum_done, 1)
                    dve.wait_ge(ksum_done, at(m, 1, 1))
                    for c in range(KC):
                        last = nc.vector.tensor_scalar(kvx[:, c, P:OW], head_of[:, :], ksum[:, c:c + 1], None, ALU.mult)
                    last.then_inc(kvx_done, 1)

                def divide(t):
                    r, half = t % 2, (t + 1) % 2
                    if t == 0:
                        dve.wait_ge(qf_done, at(m, 4, 4))
                    dve.wait_ge(o_ps, at(m, 8, t + 1))
                    bank = pb[:, half, 0:KC * OW].rearrange("p (c w) -> p c w", c=KC)
                    nc.vector.tensor_scalar(den[:, r, 0, :].rearrange("p (c h) -> p c h", c=KC), bank[:, :, P:OW],
                                            DEN_EPS, None, ALU.add).then_inc(den_done, 1)
                    dve.wait_ge(den_done, at(m, 16, 2 * t + 1))
                    nc.vector.reciprocal(den[:, r, 1, :], den[:, r, 0, :]).then_inc(den_done, 1)
                    dve.wait_ge(den_done, at(m, 16, 2 * t + 2))
                    for c in range(KC):
                        last = nc.vector.tensor_tensor(
                            out=otok[:, r, c * P:(c + 1) * P].rearrange("p (h e) -> p h e", e=DK),
                            in0=bank[:, c, 0:P].rearrange("p (h e) -> p h e", e=DK),
                            in1=den[:, r, 1, c * HPC:(c + 1) * HPC].unsqueeze(2).to_broadcast([P, HPC, DK]),
                            op=ALU.mult)
                    last.then_inc(otok_done, 1)

                pw = pb if l0 else pa

                def gate1(s):
                    rows = rows1(s)
                    slot = th1[0:rows, s % 2, :]
                    dve.wait_ge(th1_done, at(m, S1, s + 1))
                    dve.wait_ge(g1_ps, at(m, S1, s + 1))
                    nc.vector.scalar_tensor_tensor(out=slot, in0=slot, scalar=1.0, in1=pw[0:rows, 1, :],
                                                   op0=ALU.add, op1=ALU.mult).then_inc(r1_done, 1)

                def add_out(n):
                    j, c = n // KC, n % KC
                    cut = slice(j * BLK, (j + 1) * BLK)
                    dve.wait_ge(y2_ps, at(m, 4, n + 1))
                    nc.vector.scalar_tensor_tensor(out=xn1[:, c, cut], in0=pb[:, (n + 1) % 2, :],
                                                   scalar=cols[:, 3, c:c + 1], in1=x2[:, c, cut],
                                                   op0=ALU.add, op1=ALU.add).then_inc(out_done, 1)

                for g in range(GROUPS):
                    s1 = g - FFN1_G if l1 and 0 <= g - FFN1_G < S1 else None
                    if l0:
                        scan(4 * g)
                        gate0(g)
                        if g:
                            product(4 * g - 1)
                    if g == 0 and l1:
                        add_y(m, 3)
                    if l0:
                        times_gate0(g)
                        for j, f in FRONT.items():
                            if (j or more) and g == f + 1:
                                fronts[j][1](j)
                    if l1:
                        for j in range(NJ):
                            if g == TOKENS_G[j] + 1:
                                moments1(j)
                    if l0:
                        unit(4 * g + 1)
                        for j, f in FRONT.items():
                            if (j or more) and g - f - 2 in (0, 1):
                                fronts[j][2](j, g - f - 2)
                    if l1:
                        for j in range(NJ):
                            if g == TOKENS_G[j] + 1:
                                normalise1(j)
                            if g == TOKENS_G[j] + 2:
                                low_part1(j)
                        for t in range(2 * (g - KV_G - 1), 2 * (g - KV_G)):
                            if 0 <= t < NT:
                                k_feature(t)
                        if g == KV_G + 5:
                            head_blocks()
                        for n in ADD_OUT.get(g, ()):
                            add_out(n)
                    if s1 is not None and s1:
                        gate1(s1)
                    if l0:
                        unit(4 * g + 2)
                        if g and g % 4 == 0:
                            add_y(b, g // 4 - 1)
                    if l1:
                        if 0 <= g - ATTEND_G < NT // 2:
                            divide(2 * (g - ATTEND_G))
                    if l0:
                        unit(4 * g + 3)
                    if l1:
                        for t in range(2 * (g - KV_G), 2 * (g - KV_G) + 2):
                            if 0 <= t < NT:
                                kv_bias(t)
                        if 0 <= g - ATTEND_G < NT // 2:
                            divide(2 * (g - ATTEND_G) + 1)
                        if s1 == 0:
                            gate1(0)
                    if l0:
                        for j, f in FRONT.items():
                            if (j or more) and g == f:
                                fronts[j][0](j)
                        if g == GROUPS - 1:
                            product(UNITS - 1)
                            add_down(b, 0, 0)
                            add_down(b, 0, 1)
                    if l1 and g < KC:
                        add_down(m, 1, g)
                if l1:
                    add_out(3)
                    dve.wait_ge(out_done, at(m, 4, 4))

            moments0, normalise0, low_part0 = front_steps((0, 0))
            moments0(0)
            normalise0(0)
            low_part0(0, 0)
            low_part0(0, 1)
            setup()
            thresholds(0)
            quantise(0, flat(q_up), raw0[:, 0, :], KC * F0, UP_Q)
            quantise(1, flat(q_gate), raw0[:, 1, :], KC * F0, UP_Q)
            quantise(2, flat(q_down), raw0[:, 2, :], KC * F0, 1.0)
            thresholds(1)
            quantise(3, flat(q_w1), raw1[:, 0, 0:KC * F1], KC * F1, UP_Q)
            quantise(4, flat(q_w2), raw1[:, 1, 0:KC * F1], KC * F1, W2_Q)
            quantise(5, flat(q_w3), raw1[:, 2, :], RAW1, W3_Q)
            body(0, True, False, True, first=True)
            with dve.Fori(1, NBATCH - 1) as i:
                body(i, True, True, True)
            body(NBATCH - 1, True, True, False)
            body(NBATCH, False, True, False)

        @block.tensor
        def _(pe):
            mm = nc.tensor.matmul

            def wide(bank, w, f, rows, high, low, done):
                n = 0
                for k in range(KC):
                    for part in (high, low):
                        last = mm(bank[0:rows, :], w[:, k, f * P:f * P + rows], part[k],
                                  start=(n == 0), stop=(n == 2 * KC - 1))
                        n += 1
                last.then_inc(done, 1)

            def front_steps(b):
                def to_channels0(j, c):
                    if c == 0:
                        pe.wait_ge(xn_tok0, at(b, 8, 4 * j + 4))
                        wait(pe, pre_free, at(b, 4, 2 * j))
                    else:
                        pe.wait_ge(xl_done0, at(b, 4, 2 * j + 1))
                    for t in range(BT):
                        last = nc.tensor.transpose(pf[:, t * P:(t + 1) * P], xtok[:, t, c * P:(c + 1) * P],
                                                   ident[:, :])
                    last.then_inc(xnt_ps0, 1)

                def low(j):
                    pe.wait_ge(xl_done0, at(b, 4, 2 * j + 2))
                    for k in range(KC):
                        last = mm(pf[0:RANK + 2 * NS, :], win_sb[:, k, :], xn0[:, j, k, :],
                                  start=(k == 0), stop=(k == KC - 1))
                    last.then_inc(low_ps, 1)

                def pre(j, c):
                    pe.wait_ge(low_sb, at(b, 2, j + 1))
                    if c:
                        pe.wait_ge(pre_free, at(b, 4, 2 * j + 1))
                    mm(pf[:, :], wdt_sb[:, c * P:(c + 1) * P], lbc[0:RANK, :], start=True, stop=True)\
                        .then_inc(pre_ps, 1)

                return to_channels0, low, pre

            def body(i, l0, l1, more, first=False):
                b, m = (i, 0), (i, 1)
                fronts = {1: front_steps(b), 0: front_steps((i, -1))}

                def gated0(b, s):
                    j, f = s // FT0, s % FT0
                    high, low_ = [xh0[:, j, k, :] for k in range(KC)], [xl0[:, j, k, :] for k in range(KC)]
                    if s == 0:
                        pe.wait_ge(xl_done0, at(b, 4, 2))
                    elif s == FT0:
                        pe.wait_ge(xl_done0, at(b, 4, 4))
                    wait(pe, t1_done, at(b, S0, s))
                    wide(pa[:, 0, :], q_up, f, P, high, low_, u0_ps)
                    wait(pe, r0_done, at(b, S0, s))
                    wide(pa[:, 1, :], q_gate, f, P, high, low_, g0_ps)

                def skip(k):
                    if k or not first:
                        wait(pe, y_free, at(b, 4, k))
                    for q in range(NQ):
                        mm(y[q * CB:(q + 1) * CB, :], diag_d[:, k % KC, q * CB:(q + 1) * CB], xn0[:, k // KC, k % KC, :],
                           start=True, stop=False, tile_position=(0, q * CB))

                def reduce(b, g):
                    pe.wait_ge(prod_done, at(b, UNITS, 4 * g + 4))
                    for q in range(NQ):
                        last = mm(y[q * CB:(q + 1) * CB, :], reduce_w[:, :], prod[:, (4 * g + q) % PROD, :],
                                  start=False, stop=(g % 4 == 3), tile_position=(0, q * CB))
                    last.then_inc(red_done, 1)

                def down0(b, j, c):
                    if c == 0:
                        pe.wait_ge(lo0_done, at(b, S0, (j + 1) * FT0))
                    if j:
                        pe.wait_ge(x2_done, at(b, 4, c + 1))
                    elif l1:
                        pe.wait_ge(kvx_done, at(m, 1, 1))
                    for f in range(FT0):
                        for w in range(2):
                            last = mm(acc[:, c, :], q_down[:, f, c * P:(c + 1) * P],
                                      hid0[:, slot0(j * FT0 + f), w, :],
                                      start=(f == 0 and w == 0), stop=(f == FT0 - 1 and w == 1))
                    last.then_inc(down_ps, 1)

                pw = pb if l0 else pa

                def bank_of_step(bank, g):
                    pe.wait_ge((th1_done, r1_done)[bank], at(m, S1, g - FFN1_G + 1))

                def to_tokens(p):
                    pe.wait_ge(x2_done, at(m, 4, 2 if p < 2 else 4))
                    if p >= 2 and not l0:
                        pe.wait_ge(xl_done1, at(m, 4, p - 1))
                    if p == 0:
                        pe.wait_ge(y_free, at(m, 4, 4))
                    if p >= 2 and l0:
                        bank_of_step(p % 2, TOKENS_G[1])
                    for t in range(2):
                        for c in range(KC):
                            tok = (2 * p + t) * P
                            last = nc.tensor.transpose(pb[:, p % 2, (t * KC + c) * P:(t * KC + c + 1) * P],
                                                       x2[:, c, tok:tok + P], ident[:, :])
                    last.then_inc(x2_ps, 1)

                def to_channels1(j):
                    pe.wait_ge(xn_tok1, at(m, 8, 4 * j + 4))
                    for c in range(KC):
                        if j:
                            pe.wait_ge(kv_sb, at(m, 8, c + 1))
                        for t in range(BT):
                            last = nc.tensor.transpose(pb[:, c, t * P:(t + 1) * P],
                                                       x2tok[:, BT * j + t, c * P:(c + 1) * P], ident[:, :])
                        last.then_inc(xnt_ps1, 1)

                def q_proj(n):
                    c, j = n % 2, n // 2
                    if l0:
                        bank_of_step(n % 2, Q_G + n // 2)
                    elif n < 2:
                        pe.wait_ge(xl_done1, at(m, 4, 4))
                        pe.wait_ge(kv_sb, at(m, 8, 7 + n))
                    else:
                        pe.wait_ge(q_read, at(m, 4, n - 1))
                    for k in range(KC):
                        last = mm(pb[:, n % 2, :], wq_sb[:, k, c * P:(c + 1) * P],
                                  xn1[:, k, j * BLK:(j + 1) * BLK], start=(k == 0), stop=(k == KC - 1))
                    last.then_inc(q_ps, 1)

                def kv_proj(t):
                    if l0:
                        bank_of_step(t % 2, KV_G + t // 2)
                    elif t < 2:
                        pe.wait_ge(x2_tok, at(m, 4, 3 + t))
                    elif t < 4:
                        pe.wait_ge(xl_done1, at(m, 4, 1 + t))
                    else:
                        pe.wait_ge(kv_sb, at(m, 8, t - 1))
                    for k in range(KC):
                        last = mm(pb[:, t % 2, :], xn1[:, k, t * P:(t + 1) * P], wkv_sb[:, k, :],
                                  start=(k == 0), stop=(k == KC - 1))
                    last.then_inc(kv_ps, 1)

                def kv_sum(t):
                    pe.wait_ge(kf_done, at(m, 8, t + 1))
                    for c in range(KC):
                        last = mm(acc[:, c, 0:P + 1], kf[:, t % 2, c * P:(c + 1) * P], vx[:, t % 2, c, :],
                                  start=(t == 0), stop=(t == NT - 1))
                    last.then_inc(kv_acc, 1)

                def gated1(s):
                    j, f = s // FT1, s % FT1
                    cut = slice(j * BLK, (j + 1) * BLK)
                    high, low_ = [xh1[:, k, cut] for k in range(KC)], [xl1[:, k, cut] for k in range(KC)]
                    g = s + FFN1_G
                    for bank, w, done in ((0, q_w1, u1_ps), (1, q_w2, g1_ps)):
                        if not l0 and s:
                            pe.wait_ge((th1_done, r1_done)[bank], at(m, S1, s))
                            if s == FT1:
                                pe.wait_ge(xl_done1, at(m, 4, 4))
                        elif not l0:
                            pe.wait_ge(xl_done1, at(m, 4, 2))
                            pe.wait_ge(r0_done, at(m, S0, S0))
                        elif g == TOKENS_G[1]:
                            pe.wait_ge(xl_done1, at(m, 4, 2))
                        elif g == TOKENS_G[1] + 1:
                            pe.wait_ge(x2_tok, at(m, 4, 3 + bank))
                        elif g == TOKENS_G[1] + 2:
                            pe.wait_ge(xl_done1, at(m, 4, 3 + bank))
                        elif g <= Q_G:
                            pe.wait_ge(kv_sb, at(m, 8, 2 * (g - KV_G) - 1 + bank))
                        elif g <= ATTEND_G:
                            pe.wait_ge(q_read, at(m, 4, 2 * (g - Q_G) - 1 + bank))
                        else:
                            pe.wait_ge(otok_done, at(m, 8, 2 * (g - ATTEND_G) - bank))
                        wide(pw[:, bank, :], w, f, rows1(s), high, low_, done)

                def attend(t):
                    if t == 0:
                        pe.wait_ge(kvx_done, at(m, 1, 1))
                    if t % BT == 0:
                        pe.wait_ge(qf_done, at(m, 4, 2 + 2 * (t // BT)))
                    if t < 2 and not l0:
                        pe.wait_ge(q_read, at(m, 4, 4 - t))
                    elif t % 2 == 0 and not l0:
                        pe.wait_ge(otok_done, at(m, 8, t - 1))
                    elif t % 2 == 0:
                        pe.wait_ge(r1_done, at(m, S1, ATTEND_G + t // 2 - FFN1_G + 1))
                    elif t == 1:
                        pe.wait_ge(th1_done, at(m, S1, ATTEND_G - FFN1_G + 1))
                    else:
                        pe.wait_ge(ot_done, at(m, 4, t // 2))
                    for c in range(KC):
                        last = mm(pb[:, (t + 1) % 2, c * OW:(c + 1) * OW], qf[:, c, t * P:(t + 1) * P], kvx[:, c, :],
                                  start=True, stop=True)
                    last.then_inc(o_ps, 1)

                def back(p):
                    pe.wait_ge(otok_done, at(m, 8, 2 * p + 2))
                    if l0:
                        pe.wait_ge(th1_done, at(m, S1, ATTEND_G + 1 + p - FFN1_G + 1))
                    for c in range(KC):
                        for r in range(2):
                            last = nc.tensor.transpose(pb[:, 0, (c * 2 + r) * P:(c * 2 + r + 1) * P],
                                                       otok[:, r, c * P:(c + 1) * P], ident[:, :])
                    last.then_inc(ot_ps, 1)

                def outputs1(n):
                    j, c = n // KC, n % KC
                    bank, cut = pb[:, (n + 1) % 2, :], slice(j * BLK, (j + 1) * BLK)
                    if c == 0:
                        pe.wait_ge(lo1_done, at(m, S1, (j + 1) * FT1))
                    if n < 2:
                        pe.wait_ge(ot_done, at(m, 4, 2 * n + 2))
                    if n == 0:
                        pe.wait_ge(r1_done, at(m, S1, S1))
                    elif n >= 2:
                        pe.wait_ge(out_done, at(m, 4, n - 1))
                    for k in range(KC):
                        mm(bank, wo_sb[:, k, c * P:(c + 1) * P], qf[:, k, cut], start=(k == 0), stop=False)
                    for f in range(FT1):
                        rows = rows1(f)
                        for w in range(2):
                            last = mm(bank, q_w3[0:rows, f, c * P:(c + 1) * P],
                                      hid1[0:rows, j * FT1 + f, w, :], start=False, stop=(f == FT1 - 1 and w == 1))
                    last.then_inc(y2_ps, 1)

                for g in range(GROUPS):
                    s1 = g - FFN1_G if l1 and 0 <= g - FFN1_G < S1 else None
                    if l0:
                        if g == 0 and first:
                            gated0(b, 0)
                    if g == 0 and l1:
                        reduce(m, GROUPS - 1)
                    if l1 and g < KC:
                        down0(m, 1, g)
                    if l1:
                        if g == TOKENS_G[0]:
                            to_tokens(0)
                            to_tokens(1)
                    if s1 is not None and s1:
                        gated1(s1)
                    if l0:
                        if g:
                            if (g - 1) % 4 == 0:
                                skip((g - 1) // 4)
                            reduce(b, g - 1)
                    if l1:
                        for t in range(2 * (g - KV_G - 1), 2 * (g - KV_G)):
                            if 0 <= t < NT:
                                kv_sum(t)
                        for t in range(2 * (g - KV_G), 2 * (g - KV_G) + 2):
                            if 0 <= t < NT:
                                kv_proj(t)
                    if l0:
                        if g + 1 < GROUPS:
                            gated0(b, g + 1)
                        elif more:
                            gated0((i, -1), 0)
                    if l1:
                        for n in range(2 * (g - Q_G), 2 * (g - Q_G) + 2):
                            if 0 <= n < 4:
                                q_proj(n)
                        if 0 <= g - ATTEND_G - 1 < NT // 2:
                            back(g - ATTEND_G - 1)
                        if 0 <= g - ATTEND_G < NT // 2:
                            attend(2 * (g - ATTEND_G))
                            attend(2 * (g - ATTEND_G) + 1)
                        for n in OUT_GROUPS.get(g, ()):
                            outputs1(n)
                    if l0:
                        if g - DOWN_G in (0, 1):
                            down0(b, 0, g - DOWN_G)
                        for j, f in FRONT.items():
                            to_channels0, low, pre = fronts[j]
                            if (j or more) and g - f - 1 in (0, 1):
                                to_channels0(j, g - f - 1)
                            if (j or more) and g == f + 3:
                                low(j)
                            if (j or more) and g - f - 4 in (0, 1):
                                pre(j, g - f - 4)
                    if l1:
                        for j in range(NJ):
                            if g == TOKENS_G[j] + 1:
                                to_channels1(j)
                        if g == TOKENS_G[1]:
                            gated1(0)
                            to_tokens(2)
                            to_tokens(3)

            to_channels0, low, pre = front_steps((0, 0))
            def weight_sums(layer):
                pe.wait_ge(const_set, 1)
                pe.wait_ge(abs_done, 3 * layer + 3)
                three = slice(3 * layer, 3 * layer + 3)
                mm(y[:, three], ones, scale_sb[:, 0, three], start=True, stop=True).then_inc(sums_ps, 1)

            pe.wait_ge(w_small, 11 * 16)
            to_channels0(0, 0)
            to_channels0(0, 1)
            low(0)
            weight_sums(0)
            pre(0, 0)
            pre(0, 1)
            pe.wait_ge(setup_dve, 2)
            weight_sums(1)
            pe.wait_ge(quant, 4)
            pe.wait_ge(w_attn, 4 * 16)
            body(0, True, False, True, first=True)
            with pe.Fori(1, NBATCH - 1) as i:
                body(i, True, True, True)
            body(NBATCH - 1, True, True, False)
            body(NBATCH, False, True, False)


def kernel(**inputs):
    import numpy as np
    import concourse.bacc as bacc
    from concourse.bass_utils import run_bass_kernel_spmd

    a = {k: np.asarray(v) for k, v in inputs.items()}
    put = np.ascontiguousarray
    x = a["L0_attn_input"]
    chan, row = np.arange(P), np.arange(P)
    arrays = {
        "x_tok": put(x),
        "x_cm": put(x.transpose(0, 2, 1)),
        "w_in": put(np.concatenate([a["L0_attn_W_dt_in"], a["L0_attn_W_B"], a["L0_attn_W_C"]]).T),
        "w_dt_out": put(a["L0_attn_W_dt_out"].T),
        "b_dt": put(a["L0_attn_b_dt_out"]),
        "d_skip": put(a["L0_attn_D"]),
        "a_log": put(a["L0_attn_A_log"].reshape(KC * NQ, CB, NSB, SB).transpose(1, 3, 0, 2).reshape(P, -1)),
        "w_up": put(a["L0_ffn_W_up"].T), "w_gate": put(a["L0_ffn_W_gate"].T), "w_down": put(a["L0_ffn_W_down"].T),
        "wq": put(a["L1_attn_wq"].T), "bq": put(a["L1_attn_bq"]),
        "wkv": put(np.concatenate([a["L1_attn_wk"], a["L1_attn_wv"]]).T),
        "bkv": put(np.concatenate([a["L1_attn_bk"], a["L1_attn_bv"]])),
        "wo": put(a["L1_attn_wo"].T), "bo": put(a["L1_attn_bo"]),
        "w1": put(a["L1_ffn_w1"].T), "w2": put(a["L1_ffn_w2"].T), "w3": put(a["L1_ffn_w3"].T),
        "ident": np.eye(P, dtype=np.float32),
        "reduce": put((chan[:, None] // SB == np.arange(CB)[None, :]).astype(np.float32)),
        "heads": put((chan[:, None] // DK == row[None, :] // DK).astype(np.float32)),
        "head_of": put((chan[:, None] // DK == np.arange(HPC)[None, :]).astype(np.float32)),
    }
    nc = bacc.Bacc("TRN2", target_bir_lowering=False, num_devices=1, dynamic_dma_scratch_size=1024)
    args = [nc.dram_tensor(f"in_{k}", v.shape, mybir.dt.from_np(v.dtype), kind="ExternalInput").ap()
            for k, v in arrays.items()]
    out = nc.dram_tensor("out_cm", (NBATCH, H, T), mybir.dt.float32, kind="ExternalOutput").ap()
    two_layer_kernel(nc, *args, out)
    r = run_bass_kernel_spmd(nc, [{f"in_{k}": v for k, v in arrays.items()}], core_ids=[0])
    return np.ascontiguousarray(r.results[0]["out_cm"].transpose(0, 2, 1))
```
